# Optimizing a Trainium2 kernel written in Bass

```python
import numpy as np
import jax
import jax.numpy as jnp

def _softmax(x, axis=-1):
    return jax.nn.softmax(x, axis=axis)

def _gelu(x):
    return jax.nn.gelu(x, approximate=True)

def _silu(x):
    return jax.nn.silu(x)

def _sigmoid(x):
    return jax.nn.sigmoid(x)

def _layernorm(x, axis=-1, eps=1e-05):
    m = jnp.mean(x, axis=axis, keepdims=True)
    v = jnp.var(x, axis=axis, keepdims=True)
    return (x - m) / jnp.sqrt(v + eps)

def _scatter_add(tgt, idx, src, axis=0):
    return tgt.at[idx].add(src)

def _segment_sum(src, seg, n):
    return jax.ops.segment_sum(src, seg, n)
kernel_name = 'mk_adj_resnorm_d4_adj_r2_7174a9'

def setup_inputs(seed: int=0):
    np.random.seed(seed)
    _w = jnp.asarray

    def _rec_inputs():
        import jax
        import jax.numpy as jnp
        _gk = jax.random.key(seed)
        x = 7.22e-05 + 1 * jax.random.normal(jax.random.fold_in(_gk, 1), (64, 128, 256), jnp.float32)
        _a = jax.random.bernoulli(jax.random.fold_in(_gk, 2), 0.03125, (64, 128, 128))
        _a = jnp.logical_or(_a, jnp.swapaxes(_a, -1, -2))
        _a = jnp.logical_or(_a, jnp.eye(128, dtype=bool))
        _af = _a.astype(jnp.float32)
        _af = _af * jax.random.uniform(jax.random.fold_in(_gk, 3), (64, 128, 128), jnp.float32, 0.05, 1)
        adj = _af
        return (x, adj)
    x, adj = _rec_inputs()

    def _L0_gnn_setup():
        import jax, jax.numpy as jnp
        import numpy as np
        EMBED_DIM = 256
        NUM_HEADS = 8
        HEAD_DIM = EMBED_DIM // NUM_HEADS
        SCALE = HEAD_DIM ** (-0.5)
        B, S = (16, 512)
        key = jax.random.key(seed)
        ks = jax.random.split(key, 12)
        init = lambda k, shape: jax.random.normal(k, shape, dtype=jnp.float32) * EMBED_DIM ** (-0.5)
        return {'x': jax.random.normal(ks[0], (B, S, EMBED_DIM), dtype=jnp.float32), 'adj_matrix': jax.random.uniform(ks[1], (B, S, S), dtype=jnp.float32), 'bond_matrix': jax.random.uniform(ks[2], (B, S, S), dtype=jnp.float32), 'Wq': init(ks[3], (EMBED_DIM, EMBED_DIM)), 'bq': jnp.zeros((EMBED_DIM,), jnp.float32), 'Wk': init(ks[4], (EMBED_DIM, EMBED_DIM)), 'bk': jnp.zeros((EMBED_DIM,), jnp.float32), 'Wv': init(ks[5], (EMBED_DIM, EMBED_DIM)), 'bv': jnp.zeros((EMBED_DIM,), jnp.float32), 'Wo': init(ks[6], (EMBED_DIM, EMBED_DIM)), 'bo': jnp.zeros((EMBED_DIM,), jnp.float32), 'seq_len': S}
    _L0_gnn_all = _L0_gnn_setup()
    _L0_gnn_in = {k: v for k, v in _L0_gnn_all.items() if k in ('Wq', 'bq', 'Wk', 'bk', 'Wv', 'bv', 'Wo', 'bo')}
    del _L0_gnn_all

    def _L1_gnn_setup():
        import jax, jax.numpy as jnp
        import numpy as np
        B, N, D_IN, D_OUT = (4, 2048, 256, 256)
        key = jax.random.key(seed)
        k1, k2, k3, k4 = jax.random.split(key, 4)
        x = jax.random.normal(k1, (B, N, D_IN), dtype=jnp.float32)
        A_shape = jax.random.uniform(k2, (B, N, N), dtype=jnp.float32)
        w = jax.random.normal(k3, (D_IN, D_OUT), dtype=jnp.float32)
        a = jax.random.normal(k4, (D_OUT,), dtype=jnp.float32)
        return {'x': x, 'A_shape': A_shape, 'w': w, 'a': a}
    _L1_gnn_all = _L1_gnn_setup()
    _L1_gnn_in = {k: v for k, v in _L1_gnn_all.items() if k in ('w', 'a')}
    del _L1_gnn_all

    def _L2_gnn_setup():
        import jax, jax.numpy as jnp
        import numpy as np
        B, N, D = (8, 1024, 256)
        key = jax.random.key(seed)
        ks = jax.random.split(key, 8)
        scale = 0.5 / np.sqrt(D)
        x = jax.random.normal(ks[0], (B, N, D), dtype=jnp.float32)
        adj = jax.random.uniform(ks[1], (B, N, N), dtype=jnp.float32)
        Wq_w = jax.random.normal(ks[2], (D, D), dtype=jnp.float32) * scale
        Wk_w = jax.random.normal(ks[3], (D, D), dtype=jnp.float32) * scale
        Wv_w = jax.random.normal(ks[4], (D, D), dtype=jnp.float32) * scale
        Wq_b = jnp.zeros((D,), dtype=jnp.float32)
        Wk_b = jnp.zeros((D,), dtype=jnp.float32)
        Wv_b = jnp.zeros((D,), dtype=jnp.float32)
        return {'x': x, 'adj': adj, 'Wq_w': Wq_w, 'Wq_b': Wq_b, 'Wk_w': Wk_w, 'Wk_b': Wk_b, 'Wv_w': Wv_w, 'Wv_b': Wv_b}
    _L2_gnn_all = _L2_gnn_setup()
    _L2_gnn_in = {k: v for k, v in _L2_gnn_all.items() if k in ('Wq_w', 'Wq_b', 'Wk_w', 'Wk_b', 'Wv_w', 'Wv_b')}
    del _L2_gnn_all

    def _L3_gnn_setup():
        import jax, jax.numpy as jnp
        import numpy as np
        EPS_LN = 1e-05

        def hypergraph_conv(x, adj, W, b):
            N, C, _ = adj.shape
            H = (adj != 0).astype(x.dtype)
            w = adj.reshape(N, -1)[:, :C]
            xw = jnp.einsum('ncd,hd->nch', x, W)
            Dn = jnp.einsum('nce,ne->nc', H, w)
            Dn = jnp.where(Dn > 0, 1.0 / Dn, 0.0)
            Be = H.sum(axis=1)
            Be = jnp.where(Be > 0, 1.0 / Be, 0.0)
            m = Be[:, :, None] * jnp.einsum('nce,nch->neh', H, xw)
            out = Dn[:, :, None] * jnp.einsum('nce,neh->nch', H, m)
            return out + b

        def layer_norm(x, g, b):
            mu = jnp.mean(x, axis=-1, keepdims=True)
            var = jnp.var(x, axis=-1, keepdims=True)
            return (x - mu) * jax.lax.rsqrt(var + EPS_LN) * g + b
        key = jax.random.key(seed)
        ks = jax.random.split(key, 4)
        N, C, Din, Dh, Dout = (16, 512, 256, 512, 256)
        x = jax.random.normal(ks[0], (N, C, Din), dtype=jnp.float32)
        adj = jax.random.uniform(ks[1], (N, C, C), dtype=jnp.float32, minval=0.1, maxval=1.0)
        W1 = jax.random.normal(ks[2], (Dh, Din), dtype=jnp.float32) * (1.0 / np.sqrt(Din))
        b1 = jnp.zeros((Dh,), dtype=jnp.float32)
        gamma = jnp.ones((Dh,), dtype=jnp.float32)
        beta = jnp.zeros((Dh,), dtype=jnp.float32)
        W2 = jax.random.normal(ks[3], (Dout, Dh), dtype=jnp.float32) * (1.0 / np.sqrt(Dh))
        b2 = jnp.zeros((Dout,), dtype=jnp.float32)
        return {'x': x, 'adj': adj, 'W1': W1, 'b1': b1, 'gamma': gamma, 'beta': beta, 'W2': W2, 'b2': b2}
    _L3_gnn_all = _L3_gnn_setup()
    _L3_gnn_in = {k: v for k, v in _L3_gnn_all.items() if k in ('W1', 'b1', 'gamma', 'beta', 'W2', 'b2')}
    del _L3_gnn_all
    return {'x': x, 'adj': adj, 'L0_gnn_Wq': _L0_gnn_in['Wq'], 'L0_gnn_bq': _L0_gnn_in['bq'], 'L0_gnn_Wk': _L0_gnn_in['Wk'], 'L0_gnn_bk': _L0_gnn_in['bk'], 'L0_gnn_Wv': _L0_gnn_in['Wv'], 'L0_gnn_bv': _L0_gnn_in['bv'], 'L0_gnn_Wo': _L0_gnn_in['Wo'], 'L0_gnn_bo': _L0_gnn_in['bo'], 'L1_gnn_w': _L1_gnn_in['w'], 'L1_gnn_a': _L1_gnn_in['a'], 'L2_gnn_Wq_w': _L2_gnn_in['Wq_w'], 'L2_gnn_Wq_b': _L2_gnn_in['Wq_b'], 'L2_gnn_Wk_w': _L2_gnn_in['Wk_w'], 'L2_gnn_Wk_b': _L2_gnn_in['Wk_b'], 'L2_gnn_Wv_w': _L2_gnn_in['Wv_w'], 'L2_gnn_Wv_b': _L2_gnn_in['Wv_b'], 'L3_gnn_W1': _L3_gnn_in['W1'], 'L3_gnn_b1': _L3_gnn_in['b1'], 'L3_gnn_gamma': _L3_gnn_in['gamma'], 'L3_gnn_beta': _L3_gnn_in['beta'], 'L3_gnn_W2': _L3_gnn_in['W2'], 'L3_gnn_b2': _L3_gnn_in['b2']}

def reference(x, adj, L0_gnn_Wq, L0_gnn_bq, L0_gnn_Wk, L0_gnn_bk, L0_gnn_Wv, L0_gnn_bv, L0_gnn_Wo, L0_gnn_bo, L1_gnn_w, L1_gnn_a, L2_gnn_Wq_w, L2_gnn_Wq_b, L2_gnn_Wk_w, L2_gnn_Wk_b, L2_gnn_Wv_w, L2_gnn_Wv_b, L3_gnn_W1, L3_gnn_b1, L3_gnn_gamma, L3_gnn_beta, L3_gnn_W2, L3_gnn_b2):
    import jax
    import jax.numpy as jnp

    def _L0_gnn_ref(x, adj_matrix, bond_matrix, Wq, bq, Wk, bk, Wv, bv, Wo, bo, seq_len):
        import jax, jax.numpy as jnp
        import numpy as np
        EMBED_DIM = 256
        NUM_HEADS = 8
        HEAD_DIM = EMBED_DIM // NUM_HEADS
        SCALE = HEAD_DIM ** (-0.5)
        B, S = (16, 512)
        b = x.shape[0]

        def proj(W, bias):
            y = jnp.einsum('bse,fe->bsf', x, W) + bias
            return y.reshape(b, seq_len, NUM_HEADS, HEAD_DIM).transpose(0, 2, 1, 3)
        q, k, v = (proj(Wq, bq), proj(Wk, bk), proj(Wv, bv))
        scores = jnp.einsum('bhqd,bhkd->bhqk', q, k) * SCALE
        mask = (adj_matrix + bond_matrix)[:, None, :, :]
        scores = scores * mask
        attn = jax.nn.softmax(scores, axis=-1)
        ctx = jnp.einsum('bhqk,bhkd->bhqd', attn, v)
        ctx = ctx.transpose(0, 2, 1, 3).reshape(b, seq_len, EMBED_DIM)
        return jnp.einsum('bse,fe->bsf', ctx, Wo) + bo

    def _L1_gnn_ref(x, A_shape, w, a):
        import jax, jax.numpy as jnp
        import numpy as np
        B, N, D_IN, D_OUT = (4, 2048, 256, 256)
        y = x @ w
        s = y @ a
        A = s[..., :, None] + s[..., None, :]
        A = jnp.tanh(A / 8.0) * 8.0
        A = jnp.where(A >= 0, A, 0.1 * A)
        A = jnp.exp(A) * A_shape
        A = A / jnp.sum(A, axis=-1, keepdims=True)
        A = A * jnp.sum(A_shape, axis=-1, keepdims=True)
        out = A @ x @ w
        return out

    def _L2_gnn_ref(x, adj, Wq_w, Wq_b, Wk_w, Wk_b, Wv_w, Wv_b):
        import jax, jax.numpy as jnp
        import numpy as np
        B, N, D = (8, 1024, 256)
        query = jnp.einsum('bnd,od->bno', x, Wq_w) + Wq_b
        keyt = jnp.einsum('bnd,od->bno', x, Wk_w) + Wk_b
        value = jnp.einsum('bnd,od->bno', x, Wv_w) + Wv_b
        weight = jnp.einsum('bqd,bkd->bqk', query, keyt)
        weight = adj * jnp.exp(weight)
        weight = weight / jnp.sum(weight, axis=2, keepdims=True)
        return jnp.einsum('bqk,bkd->bqd', weight, value)

    def _L3_gnn_ref(x, adj, W1, b1, gamma, beta, W2, b2):
        import jax, jax.numpy as jnp
        import numpy as np
        EPS_LN = 1e-05

        def hypergraph_conv(x, adj, W, b):
            N, C, _ = adj.shape
            H = (adj != 0).astype(x.dtype)
            w = adj.reshape(N, -1)[:, :C]
            xw = jnp.einsum('ncd,hd->nch', x, W)
            Dn = jnp.einsum('nce,ne->nc', H, w)
            Dn = jnp.where(Dn > 0, 1.0 / Dn, 0.0)
            Be = H.sum(axis=1)
            Be = jnp.where(Be > 0, 1.0 / Be, 0.0)
            m = Be[:, :, None] * jnp.einsum('nce,nch->neh', H, xw)
            out = Dn[:, :, None] * jnp.einsum('nce,neh->nch', H, m)
            return out + b

        def layer_norm(x, g, b):
            mu = jnp.mean(x, axis=-1, keepdims=True)
            var = jnp.var(x, axis=-1, keepdims=True)
            return (x - mu) * jax.lax.rsqrt(var + EPS_LN) * g + b
        h = jax.nn.relu(hypergraph_conv(x, adj, W1, b1))
        h = layer_norm(h, gamma, beta)
        y = hypergraph_conv(h, adj, W2, b2)
        return y + x
    x = _layernorm(x + _L0_gnn_ref(x, adj, adj, L0_gnn_Wq, L0_gnn_bq, L0_gnn_Wk, L0_gnn_bk, L0_gnn_Wv, L0_gnn_bv, L0_gnn_Wo, L0_gnn_bo, 128), axis=-1)
    x = _layernorm(x + _L1_gnn_ref(x, adj, L1_gnn_w, L1_gnn_a), axis=-1)
    x = _layernorm(x + _L2_gnn_ref(x, adj, L2_gnn_Wq_w, L2_gnn_Wq_b, L2_gnn_Wk_w, L2_gnn_Wk_b, L2_gnn_Wv_w, L2_gnn_Wv_b), axis=-1)
    x = _layernorm(x + _L3_gnn_ref(x, adj, L3_gnn_W1, L3_gnn_b1, L3_gnn_gamma, L3_gnn_beta, L3_gnn_W2, L3_gnn_b2), axis=-1)
    return x

_drawn_inputs = setup_inputs


def setup_inputs(seed=0):
    import zlib

    import numpy as np

    out = dict(_drawn_inputs(seed))
    spreads = {'L0_gnn_bq': (0.0, 0.1),
     'L0_gnn_bk': (0.0, 0.1),
     'L0_gnn_bv': (0.0, 0.1),
     'L0_gnn_bo': (0.0, 0.1),
     'L2_gnn_Wq_b': (0.0, 0.1),
     'L2_gnn_Wk_b': (0.0, 0.1),
     'L2_gnn_Wv_b': (0.0, 0.1),
     'L3_gnn_b1': (0.0, 0.1),
     'L3_gnn_gamma': (1.0, 0.2),
     'L3_gnn_beta': (0.0, 0.1),
     'L3_gnn_b2': (0.0, 0.1)}
    factors = {}
    for name, (base, spread) in spreads.items():
        noise = np.random.default_rng([zlib.crc32(name.encode()), seed]).standard_normal(out[name].shape)
        drawn = base * np.exp(spread * noise) if base else spread * noise
        out[name] = jnp.asarray(drawn.astype(out[name].dtype))
    for name, factor in factors.items():
        out[name] = (out[name] * factor).astype(out[name].dtype)
    return out
```

```python
from contextlib import ExitStack

import concourse.bass as bass
from concourse import mybir

F32 = mybir.dt.float32
ALU = mybir.AluOpType
ACT = mybir.ActivationFunctionType
AX = mybir.AxisListType

A, B, C, D, E, F = range(6)
STORE = STAGES = 6


def pipeline_program(nc, x, adj, Wq, bq, Wk, bk, Wv, bv, Wo, bo, w_l1, a_l1, Wq2, bq2, Wk2, bk2,
                     Wv2, bv2, W1, b1, gamma, beta, W2, b2, out):
    GRAPHS, N, DIM = x.shape
    HID = W1.shape[0]
    HEADS = 8
    HD = DIM // HEADS
    SCALE = float(HD) ** -0.5
    EPS = 1e-5
    KD = DIM // 128
    KH = HID // 128
    PAIRS = GRAPHS // 2
    BIAS_LOADS = 10 + 4 * KD
    PREP_COPIES = 5 + KD + KH // 2 + 3
    assert N == 128 and KD == 2 and KH == 4 and GRAPHS % 2 == 0

    FIRST = STAGES + 2
    LAST = GRAPHS
    END = GRAPHS + STAGES - 1

    with ExitStack() as ctx:
        def sb(name, shape, dt=F32):
            return ctx.enter_context(nc.sbuf_tensor(name, shape, dt))

        def sem(name):
            return ctx.enter_context(nc.semaphore(name))

        ident = sb("ident", [128, 128])
        eps = sb("eps", [128, 1])
        minus_half = sb("minus_half", [128, 1])
        wqT = sb("wqT", [128, KD, DIM])
        wkT = sb("wkT", [128, KD, DIM])
        wvT = sb("wvT", [128, KD, DIM])
        woT = sb("woT", [128, KD, DIM])
        w1l = sb("w1l", [128, KD, DIM])
        wa8 = sb("wa8", [128, DIM])
        gram = sb("gram", [128, KD, DIM])
        wv2T = sb("wv2T", [128, KD, DIM + 1])
        w1T = sb("w1T", [128, KD, HID])
        w2T = sb("w2T", [128, KH, DIM])
        qk_bias = sb("qk_bias", [128, 4])
        t_bias = sb("t_bias", [128, KD])
        bv_row = sb("bv_row", [128, DIM])
        bo_row = sb("bo_row", [128, DIM])
        bv2_row = sb("bv2_row", [128, DIM + 1])
        b1_row = sb("b1_row", [128, HID])
        gamma_row = sb("gamma_row", [128, HID])
        beta_row = sb("beta_row", [128, HID])
        b2_row = sb("b2_row", [128, DIM])
        raw = [sb(f"raw{j}", [128, 1024]) for j in range(7)]
        qk_bias_raw = sb("qk_bias_raw", [128, 4])
        a_row = sb("a_row", [128, DIM])
        bq2_row = sb("bq2_row", [128, DIM])
        bk2_row = sb("bk2_row", [128, DIM])
        bias2_col = sb("bias2_col", [128, 4])
        wa_col = sb("wa_col", [128, KD])
        prep_junk = sb("prep_junk", [128, DIM])

        x0 = sb("x0", [128, 2, DIM])
        adjA = sb("adjA", [128, 2, N])
        adjC = sb("adjC", [128, 2, N])
        adjD = sb("adjD", [128, 2, N])
        adjE = sb("adjE", [128, 2, N])
        x0T = sb("x0T", [128, KD, N])
        qkT = sb("qkT", [128, 4, N])
        v = sb("v", [128, 2, HEADS, HD + 1])
        x0b = sb("x0b", [128, 2, DIM])
        masked = sb("masked", [128, HEADS, N])
        neg_max = sb("neg_max", [128, HEADS])
        probs = sb("probs", [128, 2, HEADS, N])
        probsT = sb("probsT", [128, HEADS, N])
        rsum0 = sb("rsum0", [128, HEADS, 1])
        context = sb("context", [128, HEADS, HD])
        contextT = sb("contextT", [128, KD, N])
        res1 = sb("res1", [128, DIM])
        x1 = sb("x1", [128, 2, DIM])
        s8 = sb("s8", [128, 1])
        s_junk = sb("s_junk", [128, DIM])
        adjCT = sb("adjCT", [128, N])
        th = sb("th", [128, N])
        leaky = sb("leaky", [128, N])
        e1 = sb("e1", [128, N])
        a1T = sb("a1T", [128, N])
        a1_junk = sb("a1_junk", [128, N])
        sums1 = sb("sums1", [128, 4])
        ax1T = sb("ax1T", [128, KD, N])
        res2 = sb("res2", [128, DIM])
        x2 = sb("x2", [128, 2, DIM])
        x2T = sb("x2T", [128, KD, N])
        tT = sb("tT", [128, KD, N])
        v2 = sb("v2", [128, DIM + 1])
        e2 = sb("e2", [128, N])
        w2 = sb("w2", [128, N])
        sums2 = sb("sums2", [128, 2])
        w2dT = sb("w2dT", [128, N])
        res3 = sb("res3", [128, DIM])
        x3 = sb("x3", [128, 2, DIM])
        HT = sb("HT", [128, N])
        HTB = sb("HTB", [128, N + 1])
        deg = sb("deg", [128, 8])
        M = sb("M", [128, 2, N + 1])
        dinv = sb("dinv", [128, 2, 1])
        x3_2 = sb("x3_2", [128, DIM])
        x3b = sb("x3b", [128, 2, DIM])
        mx3T = sb("mx3T", [128, KD, N])
        hpre = sb("hpre", [128, HID])
        hrel = sb("hrel", [128, HID])
        hnorm = sb("hnorm", [128, HID])
        hgam = sb("hgam", [128, HID])
        hidden = sb("hidden", [128, 2, HID])
        mhT = sb("mhT", [128, KH, N])
        res4 = sb("res4", [128, DIM])
        x4 = sb("x4", [128, 2, DIM])
        LN1, LN2, LN3, LNH, LN4 = range(5)
        stats = sb("stats", [128, 5, 6])
        mv = sb("mv", [128, 5, 2])
        vareps = sb("vareps", [128, 5, 1])
        rstd = sb("rstd", [128, 5, 1])

        ps03 = ctx.enter_context(nc.psum_tensor("ps03", [128, 4, 512], F32))
        psA, psAF = ps03[:, 2, :], ps03[:, 3, :]
        psB, psC, psD, psE = [ctx.enter_context(nc.psum_tensor(f"ps{j}", [128, 512], F32)) for j in range(4, 8)]
        slot_scores = ps03[:, :, 0:2 * N].rearrange("p b (s k) -> p b s k", s=2)
        SLOTS = [2 * (h % 4) + h // 4 for h in range(HEADS)]
        pT_bank = [ps03[:, j, :].rearrange("p (h k) -> p h k", h=HEADS // 2) for j in range(2)]

        s_wload = [sem(f"weights_loaded{j}") for j in range(7)]
        s_rows = sem("rows_loaded")
        s_const = sem("constants_set")
        s_const_pool = sem("pool_constants_set")
        s_prep_pe = sem("prep_products")
        s_prep_out = sem("prep_copied")
        s_prep_dve = sem("prep_vector")

        s_ld_x0 = [sem(f"x0_loaded{q}") for q in range(2)]
        s_ld_A = [sem(f"adjA_loaded{q}") for q in range(2)]
        s_ld_C = [sem(f"adjC_loaded{q}") for q in range(2)]
        s_ld_D = [sem(f"adjD_loaded{q}") for q in range(2)]
        s_ld_E = [sem(f"adjE_loaded{q}") for q in range(2)]
        s_st = [sem(f"out_stored{q}") for q in range(2)]

        p_x0T, p_qk, p_v, p_sc = sem("p_x0T"), sem("p_qk"), sem("p_v"), sem("p_scores")
        p_pT0, p_pT1, p_ctx, p_ctxT, p_o = sem("p_probsT0"), sem("p_probsT1"), sem("p_context"), sem("p_contextT"), sem("p_outproj")
        p_sT, p_axT, p_y1 = sem("p_sT"), sem("p_ax1T"), sem("p_y1")
        p_x2T, p_tT, p_v2, p_s2, p_wT, p_y2 = sem("p_x2T"), sem("p_tT"), sem("p_v2"), sem("p_scores2"), sem("p_w2T"), sem("p_y2")
        p_aET, p_M, p_mx, p_h = sem("p_adjET"), sem("p_M"), sem("p_mx3T"), sem("p_h")
        p_mh, p_y3 = sem("p_mhT"), sem("p_y3")
        a_x0T, a_exp, a_pT, a_ctxT = sem("a_x0T"), sem("a_probs"), sem("a_probsT"), sem("a_contextT")
        a_adjCT, a_th, a_e1, a_axT = sem("a_adjCT"), sem("a_tanh"), sem("a_e1"), sem("a_ax1T")
        a_x2T, a_e2, a_wT = sem("a_x2T"), sem("a_e2"), sem("a_w2T")
        a_M, a_mx, a_relu, a_mh = sem("a_M"), sem("a_mx3T"), sem("a_relu"), sem("a_mhT")
        d_qk, d_v, d_mask, d_max = sem("d_qk"), sem("d_v"), sem("d_masked"), sem("d_max")
        d_pT, d_rsum0, d_ctx = sem("d_probsT"), sem("d_rsum0"), sem("d_context")
        d_s8, d_leaky, d_sumA, d_sumadj, d_rA, d_ratio = sem("d_s8"), sem("d_leaky"), sem("d_sumA"), sem("d_sumadj"), sem("d_rA"), sem("d_ratio")
        d_tT, d_v2, d_w2, d_rden = sem("d_tT"), sem("d_v2"), sem("d_w2"), sem("d_rden")
        d_HT, d_wedge, d_Bg, d_Binv, d_HTB = sem("d_HT"), sem("d_wedge"), sem("d_Bguard"), sem("d_Binv"), sem("d_HTB")
        d_Dg, d_Drec, d_Dpos, d_Dinv, d_hpre = sem("d_Dguard"), sem("d_Drec"), sem("d_Dpos"), sem("d_Dinv"), sem("d_hpre")
        d_res = [sem(f"d_res{n}") for n in range(5)]
        d_stats = [sem(f"d_stats{n}") for n in range(5)]
        d_mv = [sem(f"d_mv{n}") for n in range(5)]
        d_norm = [sem(f"d_norm{n}") for n in range(5)]
        g_x0b, g_a1T, g_x3_2, g_x3b, g_gam, g_hid = sem("g_x0b"), sem("g_a1T"), sem("g_x3_2"), sem("g_x3b"), sem("g_gamma"), sem("g_hidden")
        g_vareps = [sem(f"g_vareps{n}") for n in range(5)]
        g_rstd = [sem(f"g_rstd{n}") for n in range(5)]

        def reach(eng, semaphore, count):
            if isinstance(count, int):
                count = min(count, GRAPHS)
                if count < 1:
                    return
            eng.wait_ge(semaphore, count)

        def reach16(eng, semaphore, transfers):
            if isinstance(transfers, int):
                transfers = min(transfers, PAIRS)
                if transfers < 1:
                    return
            eng.wait_ge(semaphore, 16 * transfers)

        def works(k, q, stage):
            return not isinstance(k, int) or 0 <= 2 * k + q - stage < GRAPHS

        def run_steps(eng, step, end=END):
            for i in range(FIRST):
                step(i // 2, i % 2)
            with eng.Fori(FIRST // 2, LAST // 2) as k:
                step(k, 0)
                step(k, 1)
            for i in range(LAST, end):
                step(i // 2, i % 2)

        block = ctx.enter_context(nc.Block())

        @block.sync
        def _(sp):
            for j, (W, parts) in enumerate(((Wq, KD), (Wk, KD), (Wv, KD), (Wo, KD))):
                sp.dma_start(raw[j // 2][:, 512 * (j % 2):512 * (j % 2) + 512].rearrange("p (h d) -> p h d", h=parts),
                             W.rearrange("(h p) d -> p h d", p=128)).then_inc(s_wload[j // 2], 16)
            sp.dma_start(x0[:, 0, :], x[0]).then_inc(s_ld_x0[0], 16)
            sp.dma_start(adjA[:, 0, :], adj[0]).then_inc(s_ld_A[0], 16)
            for j, W in enumerate((Wq2, Wk2)):
                sp.dma_start(raw[2][:, 512 * j:512 * j + 512].rearrange("p (h d) -> p h d", h=KD),
                             W.rearrange("(h p) d -> p h d", p=128)).then_inc(s_wload[2], 16)
            sp.dma_start(raw[3][:, 0:512].rearrange("p (h d) -> p h d", h=KD),
                         Wv2.rearrange("(h p) d -> p h d", p=128)).then_inc(s_wload[3], 16)
            sp.dma_start(raw[4][:, :].rearrange("p (h d) -> p h d", h=KH),
                         W1.rearrange("(h p) d -> p h d", p=128)).then_inc(s_wload[4], 16)
            sp.dma_start(raw[5][:, :].rearrange("p (h d) -> p h d", h=KD),
                         W2.rearrange("(h p) d -> p h d", p=128)).then_inc(s_wload[5], 16)
            sp.dma_start(w1l[:, :, :], w_l1.rearrange("(h p) f -> p h f", p=128)).then_inc(s_wload[6], 16)

            def step(k, q):
                i = 2 * k + q
                for stage, dst, src, loaded, used in (
                        (A, x0, x, s_ld_x0, g_x0b), (A, adjA, adj, s_ld_A, d_mask),
                        (C, adjC, adj, s_ld_C, d_sumadj), (D, adjD, adj, s_ld_D, d_w2),
                        (E, adjE, adj, s_ld_E, p_aET)):
                    if not works(k, q, stage) or (isinstance(k, int) and i == 0):
                        continue
                    g, half = i - stage, (q - stage) % 2
                    reach(sp, used, g - 1)
                    if dst is x0:
                        reach(sp, p_x0T, g - 1)
                    if dst is adjC:
                        reach(sp, p_sT, g - 1)
                        reach(sp, d_sumA, g - 1)
                    sp.dma_start(dst[:, half, :], src[g]).then_inc(loaded[half], 16)
                if works(k, q, STORE):
                    reach(sp, d_norm[LN4], i - STORE + 1)
                    sp.dma_start(out[i - STORE], x4[:, (q - STORE) % 2, :]).then_inc(s_st[(q - STORE) % 2], 16)

            run_steps(sp, step, END + 1)
            for q in range(2):
                sp.wait_ge(s_st[q], 16 * PAIRS)

        @block.gpsimd
        def _(pool):
            nc.gpsimd.memset(ident[:, :], 0.0).then_inc(s_const_pool, 1)
            nc.gpsimd.memset(minus_half[:, :], -0.5).then_inc(s_const_pool, 1)
            nc.gpsimd.memset(eps[:, :], EPS).then_inc(s_const_pool, 1)
            pool.wait_ge(s_const_pool, 3)
            nc.gpsimd.affine_select(out=ident[:, :], in_=ident[:, :], compare_op=ALU.not_equal, fill=1.0,
                                    base=0, pattern=[[-1, 128]], channel_multiplier=1).then_inc(s_const, 1)
            rows = ((bv_row[:, :], bv), (bo_row[:, :], bo), (bv2_row[:, 0:DIM], bv2), (b1_row[:, :], b1),
                    (gamma_row[:, :], gamma), (beta_row[:, :], beta), (b2_row[:, :], b2),
                    (a_row[:, :], a_l1), (bq2_row[:, :], bq2), (bk2_row[:, :], bk2))
            for dst, src in rows:
                pool.dma_start(dst, src.partition_broadcast(128)).then_inc(s_rows, 16)
            for dst, at, src in ((qk_bias_raw, 0, bq), (qk_bias_raw, 2, bk), (bias2_col, 0, bq2), (bias2_col, 2, bk2)):
                for h in range(KD):
                    pool.dma_start(dst[:, at + h:at + h + 1], src.rearrange("(h p o) -> h p o", p=128, o=1)[h]).then_inc(s_rows, 16)
            pool.wait_ge(s_rows, 16 * BIAS_LOADS)

            def rstd_of(n, g):
                reach(pool, d_mv[n], g + 1)
                reach(pool, g_rstd[n], g)
                nc.gpsimd.tensor_tensor(vareps[:, n, :], mv[:, n, 1:2], eps[:, :], ALU.add).then_inc(g_vareps[n], 1)
                reach(pool, g_vareps[n], g + 1)
                reach(pool, d_norm[n], g)
                nc.gpsimd.tensor_tensor(rstd[:, n, :], vareps[:, n, :], minus_half[:, :], ALU.pow).then_inc(g_rstd[n], 1)

            def step(k, q):
                i = 2 * k + q
                if works(k, q, A):
                    g, half = i - A, (q - A) % 2
                    reach16(pool, s_ld_x0[half], k + (q - A) // 2 + 1)
                    reach(pool, d_res[LN1], g - 1)
                    nc.gpsimd.tensor_tensor(x0b[:, half, :], x0[:, half, :], bo_row[:, :], ALU.add).then_inc(g_x0b, 1)
                if works(k, q, E):
                    g, half = i - E, (q - E) % 2
                    reach(pool, d_norm[LN3], g + 1)
                    reach(pool, g_x3b, g)
                    nc.gpsimd.tensor_tensor(x3_2[:, :], x3[:, half, :], x3[:, half, :], ALU.add).then_inc(g_x3_2, 1)
                    reach(pool, g_x3_2, g + 1)
                    reach(pool, d_res[LN4], g - 1)
                    nc.gpsimd.tensor_tensor(x3b[:, half, :], x3_2[:, :], b2_row[:, :], ALU.add).then_inc(g_x3b, 1)
                if works(k, q, C):
                    g, half = i - C, (q - C) % 2
                    reach(pool, a_e1, g + 1)
                    reach(pool, a_adjCT, g + 1)
                    reach(pool, p_axT, g)
                    nc.gpsimd.tensor_tensor(a1T[:, :], e1[:, :], adjCT[:, :], ALU.mult).then_inc(g_a1T, 1)
                if works(k, q, C):
                    rstd_of(LN2, i - C)
                if works(k, q, B):
                    rstd_of(LN1, i - B)
                if works(k, q, E):
                    g, half = i - E, (q - E) % 2
                    rstd_of(LNH, g)
                if works(k, q, F):
                    rstd_of(LN4, i - F)
                if works(k, q, D):
                    rstd_of(LN3, i - D)
                if works(k, q, E):
                    g, half = i - E, (q - E) % 2
                    reach(pool, d_norm[LNH], g + 1)
                    reach(pool, g_hid, g)
                    nc.gpsimd.tensor_tensor(hgam[:, :], hnorm[:, :], gamma_row[:, :], ALU.mult).then_inc(g_gam, 1)
                    reach(pool, g_gam, g + 1)
                    reach(pool, p_mh, g - 1)
                    nc.gpsimd.tensor_tensor(hidden[:, half, :], hgam[:, :], beta_row[:, :], ALU.add).then_inc(g_hid, 1)

            run_steps(pool, step)

        TR = [(wqT, 0, 0), (wkT, 0, 512), (wvT, 1, 0), (woT, 1, 512), (wv2T, 3, 0)]

        @block.tensor
        def _(pe):
            pe.wait_ge(s_const, 1)
            banks = [psA, psAF, psB, psC, psD, psE]
            n = [0]

            def prep_done(ins):
                n[0] += 1
                ins.then_inc(s_prep_pe, 1)

            def prep_bank():
                if n[0] >= len(banks):
                    pe.wait_ge(s_prep_out, n[0] - len(banks) + 1)
                return banks[n[0] % len(banks)]

            for _, j, at in TR:
                pe.wait_ge(s_wload[j], 16 if j == 3 else 32)
                bank = prep_bank()
                src = raw[j][:, at:at + 512].rearrange("p (h c d) -> p h c d", h=KD, c=KD)
                for c in range(KD):
                    for h in range(KD):
                        last = nc.tensor.transpose(bank[:, 256 * c + 128 * h:256 * c + 128 * h + 128], src[:, h, c, :], ident[:, :])
                prep_done(last)
            pe.wait_ge(s_wload[4], 16)
            src = raw[4][:, :].rearrange("p (h c d) -> p h c d", h=KH, c=KD)
            for c in range(KD):
                bank = prep_bank()
                for h in range(KH):
                    last = nc.tensor.transpose(bank[:, 128 * h:128 * h + 128], src[:, h, c, :], ident[:, :])
                prep_done(last)
            pe.wait_ge(s_wload[5], 16)
            src = raw[5][:, :].rearrange("p (h c d) -> p h c d", h=KD, c=KH)
            for cc in range(KH // 2):
                bank = prep_bank()
                for c in range(2):
                    for h in range(KD):
                        last = nc.tensor.transpose(bank[:, 256 * c + 128 * h:256 * c + 128 * h + 128], src[:, h, 2 * cc + c, :], ident[:, :])
                prep_done(last)
            pe.wait_ge(s_wload[2], 32)
            q2 = raw[2][:, 0:512].rearrange("p (h d) -> p h d", h=KD)
            k2 = raw[2][:, 512:1024].rearrange("p (h d) -> p h d", h=KD)
            bank = prep_bank()
            for c in range(KD):
                for h in range(KD):
                    last = nc.tensor.matmul(bank[:, 256 * c:256 * c + 256], q2[:, h, 128 * c:128 * c + 128], k2[:, h, :],
                                            start=(h == 0), stop=(h == KD - 1))
            prep_done(last)
            pe.wait_ge(s_rows, 16 * BIAS_LOADS)
            bank = prep_bank()
            for m, (W, b) in enumerate(((k2, 0), (q2, 2))):
                for c in range(KD):
                    for h in range(KD):
                        last = nc.tensor.matmul(bank[:, 2 * m + c:2 * m + c + 1], W[:, h, 128 * c:128 * c + 128],
                                                bias2_col[:, b + h:b + h + 1], start=(h == 0), stop=(h == KD - 1))
            prep_done(last)
            pe.wait_ge(s_prep_dve, KD)
            bank = prep_bank()
            for c in range(KD):
                last = nc.tensor.transpose(bank[:, 128 * c:128 * c + 128], wa_col[:, c:c + 1].to_broadcast([128, 128]), ident[:, :])
            prep_done(last)
            pe.wait_ge(s_prep_out, n[0])

            def step(k, q):
                i = 2 * k + q
                gA, gB, gC, gD, gE, gF = (i - s for s in range(STAGES))
                hA, hB, hC, hD, hE, hF = ((q - s) % 2 for s in range(STAGES))
                if works(k, q, A):
                    reach16(pe, s_ld_x0[hA], k + (q - A) // 2 + 1)
                    reach(pe, d_mask, gA)
                    for c in range(KD):
                        last = nc.tensor.transpose(psA[:, 128 * c:128 * c + 128], x0[:, hA, 128 * c:128 * c + 128], ident[:, :])
                    last.then_inc(p_x0T, 1)
                if works(k, q, D):
                    reach(pe, d_norm[LN2], gD + 1)
                    reach(pe, d_res[LN3], gD)
                    for c in range(KD):
                        last = nc.tensor.transpose(psD[:, 128 * c:128 * c + 128], x2[:, hD, 128 * c:128 * c + 128], ident[:, :])
                    last.then_inc(p_x2T, 1)
                if works(k, q, E):
                    reach16(pe, s_ld_E[hE], k + (q - E) // 2 + 1)
                    reach(pe, d_hpre, gE)
                    nc.tensor.transpose(psE[:, 0:N], adjE[:, hE, :], ident[:, :]).then_inc(p_aET, 1)
                if works(k, q, B):
                    reach(pe, a_exp, gB + 1)
                    for slot in range(HEADS):
                        last = nc.tensor.transpose(pT_bank[slot // 4][:, slot % 4, :], probs[:, hB, slot, :], ident[:, :])
                        if slot == 3:
                            last.then_inc(p_pT0, 1)
                    last.then_inc(p_pT1, 1)
                if works(k, q, C):
                    reach(pe, d_s8, gC + 1)
                    reach16(pe, s_ld_C[hC], k + (q - C) // 2 + 1)
                    reach(pe, d_res[LN2], gC)
                    nc.tensor.transpose(psC[:, 0:N], adjC[:, hC, :], ident[:, :])
                    nc.tensor.transpose(psC[:, N:2 * N], s8[:, :].to_broadcast([128, 128]), ident[:, :]).then_inc(p_sT, 1)
                if works(k, q, A):
                    reach(pe, a_x0T, gA + 1)
                    reach(pe, d_res[LN4], i - F)
                    for m, W in enumerate((wqT, wkT)):
                        for f in range(KD):
                            for c in range(KD):
                                last = nc.tensor.matmul(psAF[:, 256 * m + 128 * f:256 * m + 128 * f + 128],
                                                        W[:, c, 128 * f:128 * f + 128], x0T[:, c, :],
                                                        start=(c == 0), stop=(c == KD - 1))
                    last.then_inc(p_qk, 1)
                if works(k, q, D):
                    reach(pe, a_x2T, gD + 1)
                    for f in range(KD):
                        for c in range(KD):
                            last = nc.tensor.matmul(psD[:, 128 * f:128 * f + 128], gram[:, c, 128 * f:128 * f + 128], x2T[:, c, :],
                                                    start=(c == 0), stop=(c == KD - 1))
                    last.then_inc(p_tT, 1)
                if works(k, q, E):
                    reach(pe, d_HTB, gE + 1)
                    nc.tensor.matmul(psE[:, 0:N + 1], HT[:, :], HTB[:, :], start=True, stop=True).then_inc(p_M, 1)
                if works(k, q, F):
                    reach(pe, g_hid, gF + 1)
                    reach(pe, a_M, gF + 1)
                    reach(pe, d_qk, i + 1)
                    for c in range(KH):
                        last = nc.tensor.matmul(psAF[:, 128 * c:128 * c + 128], hidden[:, hF, 128 * c:128 * c + 128], M[:, hF, 0:N],
                                                start=True, stop=True)
                    last.then_inc(p_mh, 1)
                if works(k, q, A):
                    for c in range(KD):
                        last = nc.tensor.matmul(psA[:, 0:DIM], x0T[:, c, :], wvT[:, c, :], start=(c == 0), stop=(c == KD - 1))
                    last.then_inc(p_v, 1)
                if works(k, q, E):
                    reach(pe, a_M, gE + 1)
                    for c in range(KD):
                        last = nc.tensor.matmul(psE[:, 128 * c:128 * c + 128], x3[:, hE, 128 * c:128 * c + 128], M[:, hE, 0:N],
                                                start=True, stop=True)
                    last.then_inc(p_mx, 1)
                if works(k, q, B):
                    reach(pe, a_pT, gB + 1)
                    reach(pe, d_pT, gB + 1)
                    reach(pe, d_v, gB + 1)
                    reach(pe, d_res[LN1], gB)
                    for h in range(HEADS):
                        last = nc.tensor.matmul(psB[:, (HD + 1) * h:(HD + 1) * (h + 1)], probsT[:, SLOTS[h], :], v[:, hB, h, :],
                                                start=True, stop=True)
                    last.then_inc(p_ctx, 1)
                if works(k, q, C):
                    reach(pe, g_a1T, gC + 1)
                    for c in range(KD):
                        last = nc.tensor.matmul(psC[:, 128 * c:128 * c + 128], x1[:, hC, 128 * c:128 * c + 128], a1T[:, :],
                                                start=True, stop=True)
                    last.then_inc(p_axT, 1)
                if works(k, q, A):
                    reach(pe, d_qk, gA + 1)
                    reach(pe, d_v, gA + 1)
                    reach(pe, a_mh, i - F + 1)
                    reach(pe, a_pT, i - B + 1)
                    reach(pe, d_pT, i - B + 1)
                    for h in range(HEADS):
                        at = slice(HD * (h % 4), HD * (h % 4) + HD)
                        last = nc.tensor.matmul(slot_scores[:, h % 4, h // 4, :], qkT[at, h // 4, :], qkT[at, 2 + h // 4, :],
                                                start=True, stop=True)
                    last.then_inc(p_sc, 1)
                if works(k, q, D):
                    reach(pe, d_tT, gD + 1)
                    for c in range(KD):
                        last = nc.tensor.matmul(psD[:, 0:DIM + 1], x2T[:, c, :], wv2T[:, c, :], start=(c == 0), stop=(c == KD - 1))
                    last.then_inc(p_v2, 1)
                if works(k, q, E):
                    reach(pe, a_mx, gE + 1)
                    for c in range(KD):
                        last = nc.tensor.matmul(psE[:, :], mx3T[:, c, :], w1T[:, c, :], start=(c == 0), stop=(c == KD - 1))
                    last.then_inc(p_h, 1)
                if works(k, q, D):
                    reach(pe, d_v2, gD + 1)
                    for c in range(KD):
                        last = nc.tensor.matmul(psD[:, 0:N], tT[:, c, :], x2T[:, c, :], start=(c == 0), stop=(c == KD - 1))
                    last.then_inc(p_s2, 1)
                if works(k, q, B):
                    reach(pe, d_ctx, gB + 1)
                    for c in range(KD):
                        last = nc.tensor.transpose(psB[:, 128 * c:128 * c + 128],
                                                   context[:, 4 * c:4 * c + 4, :].rearrange("p h d -> p (h d)"), ident[:, :])
                    last.then_inc(p_ctxT, 1)
                if works(k, q, C):
                    reach(pe, a_axT, gC + 1)
                    for c in range(KD):
                        last = nc.tensor.matmul(psC[:, 0:DIM], ax1T[:, c, :], w1l[:, c, :], start=(c == 0), stop=(c == KD - 1))
                    last.then_inc(p_y1, 1)
                if works(k, q, B):
                    reach(pe, a_ctxT, gB + 1)
                    for c in range(KD):
                        last = nc.tensor.matmul(psB[:, 0:DIM], contextT[:, c, :], woT[:, c, :], start=(c == 0), stop=(c == KD - 1))
                    last.then_inc(p_o, 1)
                if works(k, q, D):
                    reach(pe, d_w2, gD + 1)
                    nc.tensor.transpose(psD[:, 0:N], w2[:, :], ident[:, :]).then_inc(p_wT, 1)
                if works(k, q, F):
                    reach(pe, a_mh, gF + 1)
                    reach(pe, d_mask, i + 1)
                    for c in range(KH):
                        last = nc.tensor.matmul(psAF[:, 0:DIM], mhT[:, c, :], w2T[:, c, :], start=(c == 0), stop=(c == KH - 1))
                    last.then_inc(p_y3, 1)
                if works(k, q, D):
                    reach(pe, a_wT, gD + 1)
                    nc.tensor.matmul(psD[:, 0:DIM], w2dT[:, :], v2[:, 0:DIM], start=True, stop=True).then_inc(p_y2, 1)

            run_steps(pe, step)

        @block.scalar
        def _(act):
            banks = [psA, psAF, psB, psC, psD, psE]
            dsts = [t[:, :, 0:DIM] for t, _, _ in TR] + [w1T[:, c, :] for c in range(KD)]
            dsts += [w2T[:, 2 * c:2 * c + 2, :] for c in range(KH // 2)] + [gram[:, :, :]]
            for n, dst in enumerate(dsts):
                act.wait_ge(s_prep_pe, n + 1)
                src = banks[n % len(banks)][:, :]
                if len(dst.shape) == 3:
                    src = src.rearrange("p (c f) -> p c f", c=2)
                nc.scalar.activation(dst, src, ACT.Copy, scale=2.0 * SCALE if n == 0 else 1.0).then_inc(s_prep_out, 1)
            n = len(dsts)
            act.wait_ge(s_prep_pe, n + 1)
            bank = banks[n % len(banks)]
            nc.scalar.activation(t_bias[:, :], bank[:, 0:2], ACT.Copy)
            nc.scalar.activation(wv2T[:, :, DIM:DIM + 1], bank[:, 2:4].rearrange("p (c o) -> p c o", o=1), ACT.Copy).then_inc(s_prep_out, 1)
            act.wait_ge(s_prep_pe, n + 2)
            bank = banks[(n + 1) % len(banks)]
            nc.scalar.activation(wa8[:, :], bank[:, 0:DIM], ACT.Copy, scale=0.125).then_inc(s_prep_out, 1)

            def two(t):
                return t[:, 0:2 * N].rearrange("p (c k) -> p c k", c=2)

            def step(k, q):
                i = 2 * k + q
                gA, gB, gC, gD, gE, gF = (i - s for s in range(STAGES))
                hA, hB, hC, hD, hE, hF = ((q - s) % 2 for s in range(STAGES))
                if works(k, q, A):
                    reach(act, p_x0T, gA + 1)
                    reach(act, p_v, gA)
                    nc.scalar.activation(x0T[:, :, :], two(psA), ACT.Copy).then_inc(a_x0T, 1)
                if works(k, q, D):
                    reach(act, p_x2T, gD + 1)
                    reach(act, p_s2, gD)
                    nc.scalar.activation(x2T[:, :, :], two(psD), ACT.Copy).then_inc(a_x2T, 1)
                if works(k, q, B):
                    reach(act, p_pT0, gB + 1)
                    reach(act, p_ctx, gB)
                    nc.scalar.activation(probsT[:, 0:4, :], pT_bank[0], ACT.Copy).then_inc(a_pT, 1)
                if works(k, q, C):
                    reach(act, p_sT, gC + 1)
                    reach(act, d_leaky, gC)
                    nc.scalar.activation(th[:, :], psC[:, N:2 * N], ACT.Tanh, bias=s8[:, :]).then_inc(a_th, 1)
                    reach(act, g_a1T, gC)
                    nc.scalar.activation(adjCT[:, :], psC[:, 0:N], ACT.Copy).then_inc(a_adjCT, 1)
                if works(k, q, E):
                    reach(act, p_M, gE + 1)
                    reach(act, p_mh, gE - 1)
                    reach(act, d_Dpos, gE - 1)
                    nc.scalar.activation(M[:, hE, :], psE[:, 0:N + 1], ACT.Copy).then_inc(a_M, 1)
                if works(k, q, C):
                    reach(act, d_leaky, gC + 1)
                    reach(act, d_sumA, gC)
                    nc.scalar.activation(e1[:, :], leaky[:, :], ACT.Exp, scale=8.0).then_inc(a_e1, 1)
                if works(k, q, F):
                    reach(act, p_mh, gF + 1)
                    reach(act, p_y3, gF)
                    nc.scalar.activation(mhT[:, :, :], psAF[:, :].rearrange("p (c k) -> p c k", c=KH), ACT.Copy).then_inc(a_mh, 1)
                if works(k, q, E):
                    reach(act, p_mx, gE + 1)
                    reach(act, p_h, gE)
                    nc.scalar.activation(mx3T[:, :, :], two(psE), ACT.Copy).then_inc(a_mx, 1)
                if works(k, q, C):
                    reach(act, p_axT, gC + 1)
                    reach(act, p_y1, gC)
                    nc.scalar.activation(ax1T[:, :, :], two(psC), ACT.Copy).then_inc(a_axT, 1)
                if works(k, q, B):
                    pass
                if works(k, q, A):
                    reach(act, d_max, gA + 1)
                    reach(act, p_pT1, gA - 1)
                    for h in range(4):
                        nc.scalar.activation(probs[:, hA, h, :], masked[:, h, :], ACT.Exp, bias=neg_max[:, h:h + 1])
                if works(k, q, D):
                    reach(act, p_s2, gD + 1)
                    reach(act, d_v2, gD + 1)
                    reach(act, d_w2, gD)
                    nc.scalar.activation(e2[:, :], psD[:, 0:N], ACT.Exp, bias=v2[:, DIM:DIM + 1]).then_inc(a_e2, 1)
                if works(k, q, B):
                    reach(act, p_ctxT, gB + 1)
                    reach(act, p_o, gB)
                    nc.scalar.activation(contextT[:, :, :], two(psB), ACT.Copy).then_inc(a_ctxT, 1)
                if works(k, q, E):
                    reach(act, d_hpre, gE + 1)
                    reach(act, d_norm[LNH], gE)
                    nc.scalar.activation(hrel[:, :], hpre[:, :], ACT.Relu).then_inc(a_relu, 1)
                if works(k, q, A):
                    for h in range(4, HEADS):
                        last = nc.scalar.activation(probs[:, hA, h, :], masked[:, h, :], ACT.Exp, bias=neg_max[:, h:h + 1])
                    last.then_inc(a_exp, 1)
                if works(k, q, D):
                    reach(act, p_wT, gD + 1)
                    reach(act, p_y2, gD)
                    nc.scalar.activation(w2dT[:, :], psD[:, 0:N], ACT.Copy).then_inc(a_wT, 1)

            run_steps(act, step)

        @block.vector
        def _(dve):
            nc.vector.memset(v[:, :, :, HD:HD + 1], 1.0)
            dve.wait_ge(s_wload[6], 16)
            dve.wait_ge(s_rows, 16 * BIAS_LOADS)
            for c in range(KD):
                nc.vector.tensor_tensor_reduce(prep_junk[:, :], w1l[:, c, :], a_row[:, :], 1.0, 0.0, ALU.mult, ALU.add,
                                               wa_col[:, c:c + 1]).then_inc(s_prep_dve, 1)
                dve.wait_ge(s_prep_dve, c + 1)
            nc.vector.tensor_tensor_reduce(prep_junk[:, :], bq2_row[:, :], bk2_row[:, :], 1.0, 0.0, ALU.mult, ALU.add,
                                           bv2_row[:, DIM:DIM + 1]).then_inc(s_prep_dve, 1)
            nc.vector.tensor_scalar(qk_bias[:, 0:2], qk_bias_raw[:, 0:2], 2.0 * SCALE, None, ALU.mult).then_inc(s_prep_dve, 1)
            nc.vector.tensor_copy(qk_bias[:, 2:4], qk_bias_raw[:, 2:4]).then_inc(s_prep_dve, 1)
            dve.wait_ge(s_prep_dve, KD + 3)
            dve.wait_ge(s_prep_out, PREP_COPIES)

            def norm_stats(n, g, res, width):
                reach(dve, d_mv[n], g)
                nc.vector.bn_stats(stats[:, n, :], res[:, 0:width]).then_inc(d_stats[n], 1)
                dve.wait_ge(s_const, 1)
                reach(dve, d_stats[n], g + 1)
                reach(dve, g_vareps[n], g)
                nc.vector.bn_aggr(mv[:, n, :], stats[:, n, :]).then_inc(d_mv[n], 1)

            def norm_apply(n, g, dst, res):
                reach(dve, g_rstd[n], g + 1)
                reach(dve, d_mv[n], g + 1)
                nc.vector.tensor_scalar(dst, res, mv[:, n, 0:1], rstd[:, n, :], ALU.subtract, ALU.mult).then_inc(d_norm[n], 1)

            def step(k, q):
                i = 2 * k + q
                gA, gB, gC, gD, gE, gF = (i - s for s in range(STAGES))
                hA, hB, hC, hD, hE, hF = ((q - s) % 2 for s in range(STAGES))
                if works(k, q, C):
                    reach(dve, d_norm[LN1], gC + 1)
                    reach(dve, a_th, gC)
                    reach(dve, p_sT, gC)
                    nc.vector.tensor_tensor_reduce(s_junk[:, :], x1[:, hC, :], wa8[:, :], 1.0, 0.0, ALU.mult, ALU.add,
                                                   s8[:, :]).then_inc(d_s8, 1)
                if works(k, q, E):
                    reach(dve, p_aET, gE + 1)
                    reach(dve, p_M, gE)
                    nc.vector.tensor_scalar(HT[:, :], psE[:, 0:N], 0.0, 0.0, ALU.not_equal, ALU.add,
                                            accum_out=deg[:, 0:1]).then_inc(d_HT, 1)
                    nc.vector.tensor_copy(HTB[:, N:N + 1], psE[:, 0:1]).then_inc(d_wedge, 1)
                    reach(dve, d_HT, gE + 1)
                    nc.vector.tensor_scalar(deg[:, 1:2], deg[:, 0:1], 1.0, None, ALU.max).then_inc(d_Bg, 1)
                    reach(dve, d_Bg, gE + 1)
                    nc.vector.reciprocal(deg[:, 2:3], deg[:, 1:2]).then_inc(d_Binv, 1)
                if works(k, q, B):
                    reach(dve, p_pT1, gB + 1)
                    reach(dve, p_ctx, gB)
                    nc.vector.tensor_copy(probsT[:, 4:8, :], pT_bank[1]).then_inc(d_pT, 1)
                if works(k, q, E):
                    reach(dve, d_Binv, gE + 1)
                    reach(dve, d_wedge, gE + 1)
                    nc.vector.tensor_scalar(HTB[:, 0:N], HT[:, :], deg[:, 2:3], None, ALU.mult).then_inc(d_HTB, 1)
                if works(k, q, C):
                    reach(dve, a_th, gC + 1)
                    reach(dve, a_e1, gC)
                    nc.vector.scalar_tensor_tensor(leaky[:, :], th[:, :], 0.1, th[:, :], ALU.mult, ALU.max).then_inc(d_leaky, 1)
                if works(k, q, A):
                    reach(dve, p_qk, gA + 1)
                    reach(dve, p_sc, gA)
                    nc.vector.tensor_tensor(qkT[:, :, :], psAF[:, :].rearrange("p (m k) -> p m k", m=4),
                                            qk_bias[:, :].unsqueeze(2).to_broadcast([128, 4, N]), ALU.add).then_inc(d_qk, 1)
                if works(k, q, C):
                    reach(dve, a_e1, gC + 1)
                    reach(dve, d_rA, gC)
                    nc.vector.tensor_tensor_reduce(a1_junk[:, :], e1[:, :], adjC[:, hC, :], 1.0, 0.0, ALU.mult, ALU.add,
                                                   sums1[:, 0:1]).then_inc(d_sumA, 1)
                    reach(dve, d_ratio, gC)
                    nc.vector.tensor_reduce(sums1[:, 1:2], adjC[:, hC, :], AX.X, ALU.add).then_inc(d_sumadj, 1)
                    reach(dve, d_sumA, gC + 1)
                    nc.vector.reciprocal(sums1[:, 2:3], sums1[:, 0:1]).then_inc(d_rA, 1)
                if works(k, q, D):
                    reach(dve, p_tT, gD + 1)
                    reach(dve, p_s2, gD)
                    nc.vector.tensor_tensor(tT[:, :, :], psD[:, 0:DIM].rearrange("p (m k) -> p m k", m=KD),
                                            t_bias[:, :].unsqueeze(2).to_broadcast([128, KD, N]), ALU.add).then_inc(d_tT, 1)
                if works(k, q, C):
                    reach(dve, d_rA, gC + 1)
                    reach(dve, d_sumadj, gC + 1)
                    reach(dve, d_res[LN2], gC)
                    nc.vector.tensor_tensor(sums1[:, 3:4], sums1[:, 1:2], sums1[:, 2:3], ALU.mult).then_inc(d_ratio, 1)
                if works(k, q, E):
                    reach(dve, a_M, gE + 1)
                    reach(dve, d_Dinv, gE)
                    nc.vector.tensor_scalar(deg[:, 3:4], M[:, hE, N:N + 1], 1.17549435e-38, None, ALU.max).then_inc(d_Dg, 1)
                    nc.vector.tensor_scalar(deg[:, 5:6], M[:, hE, N:N + 1], 0.0, None, ALU.is_gt).then_inc(d_Dpos, 1)
                    reach(dve, d_Dg, gE + 1)
                    nc.vector.reciprocal(deg[:, 4:5], deg[:, 3:4]).then_inc(d_Drec, 1)
                if works(k, q, A):
                    reach(dve, p_v, gA + 1)
                    reach(dve, p_ctx, gA - 1)
                    nc.vector.tensor_tensor(v[:, hA, :, 0:HD], psA[:, 0:DIM].rearrange("p (h d) -> p h d", h=HEADS),
                                            bv_row[:, :].rearrange("p (h d) -> p h d", h=HEADS), ALU.add).then_inc(d_v, 1)
                if works(k, q, E):
                    reach(dve, d_Drec, gE + 1)
                    reach(dve, d_Dpos, gE + 1)
                    reach(dve, d_res[LN4], gE - 1)
                    nc.vector.tensor_tensor(dinv[:, hE, :], deg[:, 4:5], deg[:, 5:6], ALU.mult).then_inc(d_Dinv, 1)
                if works(k, q, B):
                    reach(dve, p_ctx, gB + 1)
                    reach(dve, d_ctx, gB)
                    heads = psB[:, 0:(HD + 1) * HEADS].rearrange("p (h e) -> p h e", h=HEADS)
                    nc.vector.reciprocal(rsum0[:, :, :], heads[:, :, HD:HD + 1]).then_inc(d_rsum0, 1)
                    reach(dve, d_rsum0, gB + 1)
                    reach(dve, p_ctxT, gB)
                    nc.vector.tensor_tensor(context[:, :, :], heads[:, :, 0:HD], rsum0[:, :, :].to_broadcast([128, HEADS, HD]),
                                            ALU.mult).then_inc(d_ctx, 1)
                if works(k, q, A):
                    reach(dve, p_sc, gA + 1)
                    reach16(dve, s_ld_A[hA], k + (q - A) // 2 + 1)
                    reach(dve, a_exp, gA)
                    nc.vector.tensor_tensor(masked[:, :, :].rearrange("p (b s) k -> p b s k", s=2), slot_scores,
                                            adjA[:, hA, :].unsqueeze(1).unsqueeze(1).to_broadcast([128, 4, 2, N]),
                                            ALU.mult).then_inc(d_mask, 1)
                    reach(dve, d_mask, gA + 1)
                    nc.vector.tensor_reduce(neg_max[:, :], masked[:, :, :], AX.X, ALU.max, negate=True).then_inc(d_max, 1)
                if works(k, q, D):
                    reach(dve, p_v2, gD + 1)
                    reach(dve, p_y2, gD)
                    reach(dve, a_e2, gD)
                    nc.vector.tensor_tensor(v2[:, :], psD[:, 0:DIM + 1], bv2_row[:, :], ALU.add).then_inc(d_v2, 1)
                if works(k, q, E):
                    reach(dve, p_h, gE + 1)
                    reach(dve, d_Dinv, gE + 1)
                    reach(dve, a_relu, gE)
                    nc.vector.scalar_tensor_tensor(hpre[:, :], psE[:, :], dinv[:, hE, :], b1_row[:, :], ALU.mult, ALU.add).then_inc(d_hpre, 1)
                if works(k, q, D):
                    reach(dve, a_e2, gD + 1)
                    reach16(dve, s_ld_D[hD], k + (q - D) // 2 + 1)
                    reach(dve, p_wT, gD)
                    reach(dve, d_rden, gD)
                    nc.vector.tensor_tensor_reduce(w2[:, :], e2[:, :], adjD[:, hD, :], 1.0, 0.0, ALU.mult, ALU.add,
                                                   sums2[:, 0:1]).then_inc(d_w2, 1)
                if works(k, q, C):
                    reach(dve, p_y1, gC + 1)
                    reach(dve, d_ratio, gC + 1)
                    reach(dve, d_norm[LN2], gC)
                    nc.vector.scalar_tensor_tensor(res2[:, :], psC[:, 0:DIM], sums1[:, 3:4], x1[:, hC, :], ALU.mult, ALU.add).then_inc(d_res[LN2], 1)
                    reach(dve, d_res[LN2], gC + 1)
                    norm_stats(LN2, gC, res2, DIM)
                if works(k, q, D):
                    reach(dve, d_w2, gD + 1)
                    reach(dve, d_res[LN3], gD)
                    nc.vector.reciprocal(sums2[:, 1:2], sums2[:, 0:1]).then_inc(d_rden, 1)
                if works(k, q, B):
                    reach(dve, p_o, gB + 1)
                    reach(dve, g_x0b, gB + 1)
                    reach(dve, d_norm[LN1], gB)
                    nc.vector.tensor_tensor(res1[:, :], psB[:, 0:DIM], x0b[:, hB, :], ALU.add).then_inc(d_res[LN1], 1)
                    reach(dve, d_res[LN1], gB + 1)
                    norm_stats(LN1, gB, res1, DIM)
                if works(k, q, C):
                    reach(dve, p_x2T, gC - 1)
                    reach(dve, d_res[LN3], gC - 1)
                    norm_apply(LN2, gC, x2[:, hC, :], res2[:, :])
                if works(k, q, E):
                    reach(dve, a_relu, gE + 1)
                    norm_stats(LNH, gE, hrel, HID)
                if works(k, q, B):
                    reach(dve, p_axT, gB - 1)
                    reach(dve, d_res[LN2], gB - 1)
                    norm_apply(LN1, gB, x1[:, hB, :], res1[:, :])
                if works(k, q, F):
                    reach(dve, p_y3, gF + 1)
                    reach(dve, g_x3b, gF + 1)
                    reach(dve, d_norm[LN4], gF)
                    nc.vector.scalar_tensor_tensor(res4[:, :], psAF[:, 0:DIM], dinv[:, hF, :], x3b[:, hF, :], ALU.mult, ALU.add).then_inc(d_res[LN4], 1)
                    reach(dve, d_res[LN4], gF + 1)
                    norm_stats(LN4, gF, res4, DIM)
                if works(k, q, E):
                    reach(dve, g_gam, gE)
                    norm_apply(LNH, gE, hnorm[:, :], hrel[:, :])
                if works(k, q, D):
                    reach(dve, p_y2, gD + 1)
                    reach(dve, d_rden, gD + 1)
                    reach(dve, d_norm[LN3], gD)
                    nc.vector.scalar_tensor_tensor(res3[:, :], psD[:, 0:DIM], sums2[:, 1:2], x2[:, hD, :], ALU.mult, ALU.add).then_inc(d_res[LN3], 1)
                    reach(dve, d_res[LN3], gD + 1)
                    norm_stats(LN3, gD, res3, DIM)
                if works(k, q, F):
                    reach16(dve, s_st[hF], k + (q - F) // 2)
                    norm_apply(LN4, gF, x4[:, hF, :], res4[:, :])
                if works(k, q, D):
                    reach(dve, p_mx, gD - 1)
                    reach(dve, g_x3_2, gD - 1)
                    norm_apply(LN3, gD, x3[:, hD, :], res3[:, :])

            run_steps(dve, step)


_INS = ['x', 'adj', 'L0_gnn_Wq', 'L0_gnn_bq', 'L0_gnn_Wk', 'L0_gnn_bk', 'L0_gnn_Wv', 'L0_gnn_bv', 'L0_gnn_Wo', 'L0_gnn_bo',
        'L1_gnn_w', 'L1_gnn_a', 'L2_gnn_Wq_w', 'L2_gnn_Wq_b', 'L2_gnn_Wk_w', 'L2_gnn_Wk_b', 'L2_gnn_Wv_w', 'L2_gnn_Wv_b',
        'L3_gnn_W1', 'L3_gnn_b1', 'L3_gnn_gamma', 'L3_gnn_beta', 'L3_gnn_W2', 'L3_gnn_b2']
_OUTS = [((64, 128, 256), 'float32')]


def kernel(**inputs):
    import numpy as _np
    import concourse.bacc as _bacc
    from concourse import mybir as _mybir
    from concourse.bass_utils import run_bass_kernel_spmd as _run

    nc = _bacc.Bacc("TRN2", target_bir_lowering=False, num_devices=1)
    arrays, args = {}, []
    for name in _INS:
        a = _np.ascontiguousarray(inputs[name])
        arrays[f"in_{name}_dram"] = a
        args.append(nc.dram_tensor(f"in_{name}_dram", a.shape, _mybir.dt.from_np(a.dtype), kind="ExternalInput").ap())
    for i, (shape, dtype) in enumerate(_OUTS):
        dt = _mybir.dt.from_np(_np.dtype(dtype))
        args.append(nc.dram_tensor(f"out_{i}_dram", shape, dt, kind="ExternalOutput").ap())
    pipeline_program(nc, *args)
    r = _run(nc, [arrays], core_ids=[0])
    got = tuple(r.results[0][f"out_{i}_dram"] for i in range(len(_OUTS)))
    return got[0]
```

```python
from contextlib import ExitStack

import concourse.bass as bass
from concourse import mybir

F32 = mybir.dt.float32
F32R = mybir.dt.float32r
ALU = mybir.AluOpType
ACT = mybir.ActivationFunctionType
AX = mybir.AxisListType

A, B, C, D, E, F = range(6)
STORE = STAGES = 6


def pipeline_program(nc, x, adj, Wq, bq, Wk, bk, Wv, bv, Wo, bo, w_l1, a_l1, Wq2, bq2, Wk2, bk2,
                     Wv2, bv2, W1, b1, gamma, beta, W2, b2, out):
    GRAPHS, N, DIM = x.shape
    HID = W1.shape[0]
    HEADS = 8
    HD = DIM // HEADS
    SCALE = float(HD) ** -0.5
    EPS = 1e-5
    LOWEST = -3.4028234e38
    KD = DIM // 128
    KH = HID // 128
    PAIRS = GRAPHS // 2
    BIAS_LOADS = 10 + 4 * KD
    PREP_COPIES = 5 + KD + KH // 2 + 3
    assert N == 128 and KD == 2 and KH == 4 and GRAPHS % 2 == 0

    FIRST = STAGES + 2
    LAST = GRAPHS
    END = GRAPHS + STAGES - 1

    with ExitStack() as ctx:
        def sb(name, shape, dt=F32):
            return ctx.enter_context(nc.sbuf_tensor(name, shape, dt))

        def sem(name):
            return ctx.enter_context(nc.semaphore(name))

        ident = sb("ident", [128, 128])
        eps = sb("eps", [128, 1])
        minus_half = sb("minus_half", [128, 1])
        wqT = sb("wqT", [128, KD, DIM])
        wkT = sb("wkT", [128, KD, DIM])
        wvT = sb("wvT", [128, 2, KD, DIM], F32R)
        woT = sb("woT", [128, 2, KD, DIM], F32R)
        w1l = sb("w1l", [128, 2, KD, DIM], F32R)
        wa8 = sb("wa8", [128, DIM])
        gram = sb("gram", [128, KD, DIM])
        wv2T = sb("wv2T", [128, 2, KD, DIM + 2], F32R)
        w1T = sb("w1T", [128, 2, KD, HID], F32R)
        w2T = sb("w2T", [128, 2, KH, DIM], F32R)
        qk_bias = sb("qk_bias", [128, 4])
        t_bias = sb("t_bias", [128, KD])
        bv_row = sb("bv_row", [128, DIM])
        bo_row = sb("bo_row", [128, DIM])
        bv2_row = sb("bv2_row", [128, DIM + 1])
        b1_row = sb("b1_row", [128, HID])
        gamma_row = sb("gamma_row", [128, HID])
        beta_row = sb("beta_row", [128, HID])
        b2_row = sb("b2_row", [128, DIM])
        raw = [sb(f"raw{j}", [128, 1024]) for j in range(7)]
        qk_bias_raw = sb("qk_bias_raw", [128, 4])
        w1raw = raw[6][:, 0:512].rearrange("p (h f) -> p h f", h=KD)
        a_row = sb("a_row", [128, DIM])
        bq2_row = sb("bq2_row", [128, DIM])
        bk2_row = sb("bk2_row", [128, DIM])
        bias2_col = sb("bias2_col", [128, 4])
        wa_col = sb("wa_col", [128, KD])
        prep_junk = sb("prep_junk", [128, DIM])

        x0 = sb("x0", [128, 2, DIM])
        adjA = sb("adjA", [128, 2, N])
        adjC = sb("adjC", [128, 2, N])
        adjD = sb("adjD", [128, 2, N])
        adjE = sb("adjE", [128, 2, N])
        x0T = sb("x0T", [128, KD, N])
        x0Ts = sb("x0Ts", [128, 2, KD, N], F32R)
        qkT = sb("qkT", [128, 4, N])
        v = sb("v", [128, 2, HEADS, HD + 1])
        x0b = sb("x0b", [128, 2, DIM])
        masked = sb("masked", [128, HEADS, N])
        row_max = sb("row_max", [128, HEADS])
        neg_max = sb("neg_max", [128, HEADS])
        probs = sb("probs", [128, 2, HEADS, N])
        probsT = sb("probsT", [128, HEADS, N])
        rsum0 = sb("rsum0", [128, HEADS, 1])
        context = sb("context", [128, HEADS, HD])
        contextT = sb("contextT", [128, KD, N])
        contextTs = sb("contextTs", [128, 2, KD, N], F32R)
        res1 = sb("res1", [128, DIM])
        x1 = sb("x1", [128, 2, DIM])
        s8 = sb("s8", [128, 1])
        s_junk = sb("s_junk", [128, DIM])
        adjCT = sb("adjCT", [128, N])
        th = sb("th", [128, N])
        leaky = sb("leaky", [128, N])
        e1 = sb("e1", [128, N])
        a1T = sb("a1T", [128, N])
        a1_junk = sb("a1_junk", [128, N])
        sums1 = sb("sums1", [128, 4])
        ax1T = sb("ax1T", [128, KD, N])
        ax1Ts = sb("ax1Ts", [128, 2, KD, N], F32R)
        res2 = sb("res2", [128, DIM])
        x2 = sb("x2", [128, 2, DIM])
        x2T = sb("x2T", [128, KD, N])
        x2Ts = sb("x2Ts", [128, 2, KD, N], F32R)
        tT = sb("tT", [128, KD, N])
        v2 = sb("v2", [128, DIM + 1])
        e2 = sb("e2", [128, N])
        w2 = sb("w2", [128, N])
        sums2 = sb("sums2", [128, 2])
        w2dT = sb("w2dT", [128, N])
        res3 = sb("res3", [128, DIM])
        x3 = sb("x3", [128, 2, DIM])
        HT = sb("HT", [128, N])
        HTB = sb("HTB", [128, N + 1])
        deg = sb("deg", [128, 8])
        M = sb("M", [128, 2, N + 1])
        dinv = sb("dinv", [128, 2, 1])
        x3b = sb("x3b", [128, 2, DIM])
        mx3T = sb("mx3T", [128, KD, N])
        mx3Ts = sb("mx3Ts", [128, 2, KD, N], F32R)
        hpre = sb("hpre", [128, HID])
        hrel = sb("hrel", [128, HID])
        hnorm = sb("hnorm", [128, HID])
        hgam = sb("hgam", [128, HID])
        hidden = sb("hidden", [128, 2, HID])
        mhT = sb("mhT", [128, KH, N])
        mhTs = sb("mhTs", [128, 2, KH, N], F32R)
        res4 = sb("res4", [128, DIM])
        x4 = sb("x4", [128, 2, DIM])
        LN1, LN2, LN3, LNH, LN4 = range(5)
        stats = sb("stats", [128, 5, 6])
        mv = sb("mv", [128, 5, 2])
        vareps = sb("vareps", [128, 5, 1])
        rstd = sb("rstd", [128, 5, 1])

        ps03 = ctx.enter_context(nc.psum_tensor("ps03", [128, 4, 512], F32))
        psA, psAF = ps03[:, 2, :], ps03[:, 3, :]
        psB, psC, psD, psE = [ctx.enter_context(nc.psum_tensor(f"ps{j}", [128, 512], F32)) for j in range(4, 8)]
        slot_scores = ps03[:, :, 0:2 * N].rearrange("p b (s k) -> p b s k", s=2)
        SLOTS = [2 * (h % 4) + h // 4 for h in range(HEADS)]
        pT_bank = [ps03[:, j, :].rearrange("p (h k) -> p h k", h=HEADS // 2) for j in range(2)]

        s_wload = [sem(f"weights_loaded{j}") for j in range(7)]
        s_rows = sem("rows_loaded")
        s_const = sem("constants_set")
        s_const_pool = sem("pool_constants_set")
        s_prep_pe = sem("prep_products")
        s_prep_out = sem("prep_copied")
        s_prep_dve = sem("prep_vector")
        s_prep_low = sem("prep_low_parts")

        s_ld_x0 = [sem(f"x0_loaded{q}") for q in range(2)]
        s_ld_A = [sem(f"adjA_loaded{q}") for q in range(2)]
        s_ld_C = [sem(f"adjC_loaded{q}") for q in range(2)]
        s_ld_D = [sem(f"adjD_loaded{q}") for q in range(2)]
        s_ld_E = [sem(f"adjE_loaded{q}") for q in range(2)]
        s_st = [sem(f"out_stored{q}") for q in range(2)]

        p_x0T, p_qk, p_v, p_sc = sem("p_x0T"), sem("p_qk"), sem("p_v"), sem("p_scores")
        p_pT0, p_pT1, p_ctx, p_ctxT, p_o = sem("p_probsT0"), sem("p_probsT1"), sem("p_context"), sem("p_contextT"), sem("p_outproj")
        p_sT, p_axT, p_y1 = sem("p_sT"), sem("p_ax1T"), sem("p_y1")
        p_x2T, p_tT, p_v2, p_s2, p_wT, p_y2 = sem("p_x2T"), sem("p_tT"), sem("p_v2"), sem("p_scores2"), sem("p_w2T"), sem("p_y2")
        p_aET, p_M, p_mx, p_h = sem("p_adjET"), sem("p_M"), sem("p_mx3T"), sem("p_h")
        p_mh, p_y3 = sem("p_mhT"), sem("p_y3")
        a_exp0, a_x0T, a_exp, a_pT, a_ctxT = sem("a_probs0"), sem("a_x0T"), sem("a_probs"), sem("a_probsT"), sem("a_contextT")
        a_adjCT, a_th, a_e1, a_axT = sem("a_adjCT"), sem("a_tanh"), sem("a_e1"), sem("a_ax1T")
        a_x2T, a_e2, a_wT = sem("a_x2T"), sem("a_e2"), sem("a_w2T")
        a_M, a_mx, a_relu, a_mh = sem("a_M"), sem("a_mx3T"), sem("a_relu"), sem("a_mhT")
        d_qk, d_v, d_mask, d_max = sem("d_qk"), sem("d_v"), sem("d_masked"), sem("d_max")
        d_mask0, d_max0 = sem("d_masked0"), sem("d_max0")
        d_x3b = sem("d_x3b")
        d_rsum0, d_ctx = sem("d_rsum0"), sem("d_context")
        d_s8, d_leaky, d_sumA, d_sumadj, d_rA, d_ratio = sem("d_s8"), sem("d_leaky"), sem("d_sumA"), sem("d_sumadj"), sem("d_rA"), sem("d_ratio")
        d_tT, d_v2, d_w2, d_rden = sem("d_tT"), sem("d_v2"), sem("d_w2"), sem("d_rden")
        d_HT, d_wedge, d_Bg, d_Binv, d_HTB = sem("d_HT"), sem("d_wedge"), sem("d_Bguard"), sem("d_Binv"), sem("d_HTB")
        d_Dg, d_Drec, d_Dpos, d_Dinv, d_hpre = sem("d_Dguard"), sem("d_Drec"), sem("d_Dpos"), sem("d_Dinv"), sem("d_hpre")
        d_res = [sem(f"d_res{n}") for n in range(5)]
        d_stats = [sem(f"d_stats{n}") for n in range(5)]
        d_mv = [sem(f"d_mv{n}") for n in range(5)]
        d_norm = [sem(f"d_norm{n}") for n in range(5)]
        g_x0b, g_a1T, g_gam, g_hid = sem("g_x0b"), sem("g_a1T"), sem("g_gamma"), sem("g_hidden")
        g_x0T, g_ctxT, g_axT, g_x2T, g_mx, g_mh = sem("g_x0T"), sem("g_contextT"), sem("g_ax1T"), sem("g_x2T"), sem("g_mx3T"), sem("g_mhT")
        g_vareps = [sem(f"g_vareps{n}") for n in range(5)]
        g_rstd = [sem(f"g_rstd{n}") for n in range(5)]

        def reach(eng, semaphore, count):
            if isinstance(count, int):
                count = min(count, GRAPHS)
                if count < 1:
                    return
            eng.wait_ge(semaphore, count)

        def reach16(eng, semaphore, transfers):
            if isinstance(transfers, int):
                transfers = min(transfers, PAIRS)
                if transfers < 1:
                    return
            eng.wait_ge(semaphore, 16 * transfers)

        def works(k, q, stage):
            return not isinstance(k, int) or 0 <= 2 * k + q - stage < GRAPHS

        def run_steps(eng, step, end=END):
            for i in range(FIRST):
                step(i // 2, i % 2)
            with eng.Fori(FIRST // 2, LAST // 2) as k:
                step(k, 0)
                step(k, 1)
            for i in range(LAST, end):
                step(i // 2, i % 2)

        block = ctx.enter_context(nc.Block())

        @block.sync
        def _(sp):
            for j, (W, parts) in enumerate(((Wq, KD), (Wk, KD), (Wv, KD), (Wo, KD))):
                sp.dma_start(raw[j // 2][:, 512 * (j % 2):512 * (j % 2) + 512].rearrange("p (h d) -> p h d", h=parts),
                             W.rearrange("(h p) d -> p h d", p=128)).then_inc(s_wload[j // 2], 16)
            sp.dma_start(x0[:, 0, :], x[0]).then_inc(s_ld_x0[0], 16)
            sp.dma_start(adjA[:, 0, :], adj[0]).then_inc(s_ld_A[0], 16)
            for j, W in enumerate((Wq2, Wk2)):
                sp.dma_start(raw[2][:, 512 * j:512 * j + 512].rearrange("p (h d) -> p h d", h=KD),
                             W.rearrange("(h p) d -> p h d", p=128)).then_inc(s_wload[2], 16)
            sp.dma_start(raw[3][:, 0:512].rearrange("p (h d) -> p h d", h=KD),
                         Wv2.rearrange("(h p) d -> p h d", p=128)).then_inc(s_wload[3], 16)
            sp.dma_start(raw[4][:, :].rearrange("p (h d) -> p h d", h=KH),
                         W1.rearrange("(h p) d -> p h d", p=128)).then_inc(s_wload[4], 16)
            sp.dma_start(raw[5][:, :].rearrange("p (h d) -> p h d", h=KD),
                         W2.rearrange("(h p) d -> p h d", p=128)).then_inc(s_wload[5], 16)
            sp.dma_start(w1raw, w_l1.rearrange("(h p) f -> p h f", p=128)).then_inc(s_wload[6], 16)

            def step(k, q):
                i = 2 * k + q
                for stage, dst, src, loaded, used in (
                        (A, x0, x, s_ld_x0, g_x0b), (A, adjA, adj, s_ld_A, d_mask),
                        (C, adjC, adj, s_ld_C, d_sumadj), (D, adjD, adj, s_ld_D, d_w2),
                        (E, adjE, adj, s_ld_E, p_aET)):
                    if not works(k, q, stage) or (isinstance(k, int) and i == 0):
                        continue
                    g, half = i - stage, (q - stage) % 2
                    reach(sp, used, g - 1)
                    if dst is x0:
                        reach(sp, p_x0T, g - 1)
                    if dst is adjC:
                        reach(sp, p_sT, g - 1)
                        reach(sp, d_sumA, g - 1)
                    sp.dma_start(dst[:, half, :], src[g]).then_inc(loaded[half], 16)
                if works(k, q, STORE):
                    reach(sp, d_norm[LN4], i - STORE + 1)
                    sp.dma_start(out[i - STORE], x4[:, (q - STORE) % 2, :]).then_inc(s_st[(q - STORE) % 2], 16)

            run_steps(sp, step, END + 1)
            for q in range(2):
                sp.wait_ge(s_st[q], 16 * PAIRS)

        @block.gpsimd
        def _(pool):
            nc.gpsimd.memset(ident[:, :], 0.0).then_inc(s_const_pool, 1)
            nc.gpsimd.memset(minus_half[:, :], -0.5).then_inc(s_const_pool, 1)
            nc.gpsimd.memset(eps[:, :], EPS).then_inc(s_const_pool, 1)
            pool.wait_ge(s_const_pool, 3)
            nc.gpsimd.affine_select(out=ident[:, :], in_=ident[:, :], compare_op=ALU.not_equal, fill=1.0,
                                    base=0, pattern=[[-1, 128]], channel_multiplier=1).then_inc(s_const, 1)
            rows = ((bv_row[:, :], bv), (bo_row[:, :], bo), (bv2_row[:, 0:DIM], bv2), (b1_row[:, :], b1),
                    (gamma_row[:, :], gamma), (beta_row[:, :], beta), (b2_row[:, :], b2),
                    (a_row[:, :], a_l1), (bq2_row[:, :], bq2), (bk2_row[:, :], bk2))
            for dst, src in rows:
                pool.dma_start(dst, src.partition_broadcast(128)).then_inc(s_rows, 16)
            for dst, at, src in ((qk_bias_raw, 0, bq), (qk_bias_raw, 2, bk), (bias2_col, 0, bq2), (bias2_col, 2, bk2)):
                for h in range(KD):
                    pool.dma_start(dst[:, at + h:at + h + 1], src.rearrange("(h p o) -> h p o", p=128, o=1)[h]).then_inc(s_rows, 16)
            pool.wait_ge(s_rows, 16 * BIAS_LOADS)

            def add_eps(n, g):
                reach(pool, d_mv[n], g + 1)
                reach(pool, g_rstd[n], g)
                nc.gpsimd.tensor_tensor(vareps[:, n, :], mv[:, n, 1:2], eps[:, :], ALU.add).then_inc(g_vareps[n], 1)

            def power(n, g):
                reach(pool, g_vareps[n], g + 1)
                reach(pool, d_norm[n], g)
                nc.gpsimd.tensor_tensor(rstd[:, n, :], vareps[:, n, :], minus_half[:, :], ALU.pow).then_inc(g_rstd[n], 1)

            def low_part(full, parts, ready, users, done, g):
                reach(pool, ready, g + 1)
                reach(pool, users, g)
                nc.gpsimd.tensor_tensor(parts[:, 1], full[:, :, :], parts[:, 0].bitcast(F32), ALU.subtract).then_inc(done, 1)

            def step(k, q):
                i = 2 * k + q
                if works(k, q, D):
                    low_part(x2T, x2Ts, a_x2T, p_v2, g_x2T, i - D)
                if works(k, q, B):
                    low_part(contextT, contextTs, a_ctxT, p_o, g_ctxT, i - B)
                if works(k, q, C):
                    g, half = i - C, (q - C) % 2
                    reach(pool, a_e1, g + 1)
                    reach(pool, a_adjCT, g + 1)
                    reach(pool, p_axT, g)
                    nc.gpsimd.tensor_tensor(a1T[:, :], e1[:, :], adjCT[:, :], ALU.mult).then_inc(g_a1T, 1)
                if works(k, q, F):
                    low_part(mhT, mhTs, a_mh, p_y3, g_mh, i - F)
                if works(k, q, E):
                    low_part(mx3T, mx3Ts, a_mx, p_h, g_mx, i - E)
                if works(k, q, A):
                    low_part(x0T, x0Ts, a_x0T, p_v, g_x0T, i - A)
                if works(k, q, A):
                    g, half = i - A, (q - A) % 2
                    reach16(pool, s_ld_x0[half], k + (q - A) // 2 + 1)
                    reach(pool, d_res[LN1], g - 1)
                    nc.gpsimd.tensor_tensor(x0b[:, half, :], x0[:, half, :], bo_row[:, :], ALU.add).then_inc(g_x0b, 1)
                if works(k, q, C):
                    low_part(ax1T, ax1Ts, a_axT, p_y1, g_axT, i - C)
                if works(k, q, B):
                    add_eps(LN1, i - B)
                if works(k, q, B):
                    power(LN1, i - B)
                if works(k, q, E):
                    add_eps(LNH, i - E)
                if works(k, q, C):
                    add_eps(LN2, i - C)
                if works(k, q, E):
                    power(LNH, i - E)
                if works(k, q, C):
                    power(LN2, i - C)
                if works(k, q, F):
                    add_eps(LN4, i - F)
                if works(k, q, D):
                    add_eps(LN3, i - D)
                if works(k, q, F):
                    power(LN4, i - F)
                if works(k, q, D):
                    power(LN3, i - D)
                if works(k, q, E):
                    g, half = i - E, (q - E) % 2
                    reach(pool, d_norm[LNH], g + 1)
                    reach(pool, g_hid, g)
                    nc.gpsimd.tensor_tensor(hgam[:, :], hnorm[:, :], gamma_row[:, :], ALU.mult).then_inc(g_gam, 1)
                if works(k, q, E):
                    g, half = i - E, (q - E) % 2
                    reach(pool, g_gam, g + 1)
                    reach(pool, p_mh, g - 1)
                    nc.gpsimd.tensor_tensor(hidden[:, half, :], hgam[:, :], beta_row[:, :], ALU.add).then_inc(g_hid, 1)

            run_steps(pool, step)

        PREPARED = [(wqT[:, :, :], None), (wkT[:, :, :], None), (wvT[:, 0], wvT[:, 1]), (woT[:, 0], woT[:, 1]),
                    (wv2T[:, 0, :, 0:DIM], wv2T[:, 1, :, 0:DIM])]
        PREPARED += [(w1T[:, 0, c, :], w1T[:, 1, c, :]) for c in range(KD)]
        PREPARED += [(w2T[:, 0, 2 * c:2 * c + 2, :], w2T[:, 1, 2 * c:2 * c + 2, :]) for c in range(KH // 2)]
        PREPARED += [(gram[:, :, :], None)]
        SPLIT = [low is not None for _, low in PREPARED] + [True, False]

        TR = [(0, 0), (0, 512), (1, 0), (1, 512), (3, 0)]

        @block.tensor
        def _(pe):
            pe.wait_ge(s_const, 1)
            banks = [psA, psAF, psB, psC, psD, psE]
            n = [0]

            def prep_done(ins):
                n[0] += 1
                ins.then_inc(s_prep_pe, 1)

            def prep_bank():
                if n[0] >= len(banks):
                    pe.wait_ge(s_prep_out, n[0] - len(banks) + 1)
                    low = sum(SPLIT[0:n[0] - len(banks) + 1])
                    if low:
                        pe.wait_ge(s_prep_low, low)
                return banks[n[0] % len(banks)]

            for j, at in TR:
                pe.wait_ge(s_wload[j], 16 if j == 3 else 32)
                bank = prep_bank()
                src = raw[j][:, at:at + 512].rearrange("p (h c d) -> p h c d", h=KD, c=KD)
                for c in range(KD):
                    for h in range(KD):
                        last = nc.tensor.transpose(bank[:, 256 * c + 128 * h:256 * c + 128 * h + 128], src[:, h, c, :], ident[:, :])
                prep_done(last)
            pe.wait_ge(s_wload[4], 16)
            src = raw[4][:, :].rearrange("p (h c d) -> p h c d", h=KH, c=KD)
            for c in range(KD):
                bank = prep_bank()
                for h in range(KH):
                    last = nc.tensor.transpose(bank[:, 128 * h:128 * h + 128], src[:, h, c, :], ident[:, :])
                prep_done(last)
            pe.wait_ge(s_wload[5], 16)
            src = raw[5][:, :].rearrange("p (h c d) -> p h c d", h=KD, c=KH)
            for cc in range(KH // 2):
                bank = prep_bank()
                for c in range(2):
                    for h in range(KD):
                        last = nc.tensor.transpose(bank[:, 256 * c + 128 * h:256 * c + 128 * h + 128], src[:, h, 2 * cc + c, :], ident[:, :])
                prep_done(last)
            pe.wait_ge(s_wload[2], 32)
            q2 = raw[2][:, 0:512].rearrange("p (h d) -> p h d", h=KD)
            k2 = raw[2][:, 512:1024].rearrange("p (h d) -> p h d", h=KD)
            bank = prep_bank()
            for c in range(KD):
                for h in range(KD):
                    last = nc.tensor.matmul(bank[:, 256 * c:256 * c + 256], q2[:, h, 128 * c:128 * c + 128], k2[:, h, :],
                                            start=(h == 0), stop=(h == KD - 1))
            prep_done(last)
            pe.wait_ge(s_rows, 16 * BIAS_LOADS)
            bank = prep_bank()
            for m, (W, b) in enumerate(((k2, 0), (q2, 2))):
                for c in range(KD):
                    for h in range(KD):
                        last = nc.tensor.matmul(bank[:, 2 * m + c:2 * m + c + 1], W[:, h, 128 * c:128 * c + 128],
                                                bias2_col[:, b + h:b + h + 1], start=(h == 0), stop=(h == KD - 1))
            prep_done(last)
            pe.wait_ge(s_prep_dve, KD)
            bank = prep_bank()
            for c in range(KD):
                last = nc.tensor.transpose(bank[:, 128 * c:128 * c + 128], wa_col[:, c:c + 1].to_broadcast([128, 128]), ident[:, :])
            prep_done(last)
            pe.wait_ge(s_prep_out, n[0])
            pe.wait_ge(s_prep_low, sum(SPLIT) + 1)

            def split_product(dst, parts, chunks, weights):
                terms = [(c, l, r) for l, r in ((0, 0), (0, 1), (1, 0)) for c in range(chunks)]
                for c, l, r in terms:
                    last = nc.tensor.matmul(dst, parts[:, l, c, :], weights[:, r, c, :],
                                            start=((c, l, r) == terms[0]), stop=((c, l, r) == terms[-1]))
                return last

            def step(k, q):
                i = 2 * k + q
                gA, gB, gC, gD, gE, gF = (i - s for s in range(STAGES))
                hA, hB, hC, hD, hE, hF = ((q - s) % 2 for s in range(STAGES))
                if works(k, q, A):
                    reach16(pe, s_ld_x0[hA], k + (q - A) // 2 + 1)
                    reach(pe, d_v, gA)
                    for c in range(KD):
                        last = nc.tensor.transpose(psA[:, 128 * c:128 * c + 128], x0[:, hA, 128 * c:128 * c + 128], ident[:, :])
                    last.then_inc(p_x0T, 1)
                if works(k, q, B):
                    reach(pe, a_exp, gB + 1)
                    reach(pe, d_mask, gA)
                    for slot in range(HEADS):
                        last = nc.tensor.transpose(pT_bank[slot // 4][:, slot % 4, :], probs[:, hB, slot, :], ident[:, :])
                        if slot == 3:
                            last.then_inc(p_pT0, 1)
                    last.then_inc(p_pT1, 1)
                if works(k, q, E):
                    reach16(pe, s_ld_E[hE], k + (q - E) // 2 + 1)
                    reach(pe, d_hpre, gE)
                    nc.tensor.transpose(psE[:, 0:N], adjE[:, hE, :], ident[:, :]).then_inc(p_aET, 1)
                if works(k, q, A):
                    reach(pe, a_x0T, gA + 1)
                    reach(pe, d_res[LN4], gF)
                    for m, W in enumerate((wqT, wkT)):
                        for f in range(KD):
                            for c in range(KD):
                                last = nc.tensor.matmul(psAF[:, 256 * m + 128 * f:256 * m + 128 * f + 128],
                                                        W[:, c, 128 * f:128 * f + 128], x0T[:, c, :],
                                                        start=(c == 0), stop=(c == KD - 1))
                    last.then_inc(p_qk, 1)
                if works(k, q, D):
                    reach(pe, d_norm[LN2], gD + 1)
                    reach(pe, d_res[LN3], gD)
                    for c in range(KD):
                        last = nc.tensor.transpose(psD[:, 128 * c:128 * c + 128], x2[:, hD, 128 * c:128 * c + 128], ident[:, :])
                    last.then_inc(p_x2T, 1)
                if works(k, q, B):
                    reach(pe, a_pT, gB + 1)
                    reach(pe, d_v, gB + 1)
                    reach(pe, d_res[LN1], gB)
                    for h in range(HEADS):
                        last = nc.tensor.matmul(psB[:, (HD + 1) * h:(HD + 1) * (h + 1)], probsT[:, SLOTS[h], :], v[:, hB, h, :],
                                                start=True, stop=True)
                    last.then_inc(p_ctx, 1)
                if works(k, q, C):
                    reach(pe, d_s8, gC + 1)
                    reach16(pe, s_ld_C[hC], k + (q - C) // 2 + 1)
                    reach(pe, d_res[LN2], gC)
                    nc.tensor.transpose(psC[:, 0:N], adjC[:, hC, :], ident[:, :])
                    nc.tensor.transpose(psC[:, N:2 * N], s8[:, :].to_broadcast([128, 128]), ident[:, :]).then_inc(p_sT, 1)
                if works(k, q, D):
                    reach(pe, a_x2T, gD + 1)
                    for f in range(KD):
                        for c in range(KD):
                            last = nc.tensor.matmul(psD[:, 128 * f:128 * f + 128], gram[:, c, 128 * f:128 * f + 128], x2T[:, c, :],
                                                    start=(c == 0), stop=(c == KD - 1))
                    last.then_inc(p_tT, 1)
                if works(k, q, B):
                    reach(pe, d_ctx, gB + 1)
                    for c in range(KD):
                        last = nc.tensor.transpose(psB[:, 128 * c:128 * c + 128],
                                                   context[:, 4 * c:4 * c + 4, :].rearrange("p h d -> p (h d)"), ident[:, :])
                    last.then_inc(p_ctxT, 1)
                if works(k, q, E):
                    reach(pe, d_HTB, gE + 1)
                    nc.tensor.matmul(psE[:, 0:N + 1], HT[:, :], HTB[:, :], start=True, stop=True).then_inc(p_M, 1)
                if works(k, q, F):
                    reach(pe, g_hid, gF + 1)
                    reach(pe, a_M, gF + 1)
                    reach(pe, d_qk, gA + 1)
                    for c in range(KH):
                        last = nc.tensor.matmul(psAF[:, 128 * c:128 * c + 128], hidden[:, hF, 128 * c:128 * c + 128], M[:, hF, 0:N],
                                                start=True, stop=True)
                    last.then_inc(p_mh, 1)
                if works(k, q, D):
                    reach(pe, g_x2T, gD + 1)
                    reach(pe, d_tT, gD + 1)
                    last = split_product(psD[:, 0:DIM + 2], x2Ts, KD, wv2T)
                    last.then_inc(p_v2, 1)
                if works(k, q, E):
                    reach(pe, d_norm[LN3], gE + 1)
                    reach(pe, a_M, gE + 1)
                    for c in range(KD):
                        last = nc.tensor.matmul(psE[:, 128 * c:128 * c + 128], x3[:, hE, 128 * c:128 * c + 128], M[:, hE, 0:N],
                                                start=True, stop=True)
                    last.then_inc(p_mx, 1)
                if works(k, q, B):
                    reach(pe, g_ctxT, gB + 1)
                    last = split_product(psB[:, 0:DIM], contextTs, KD, woT)
                    last.then_inc(p_o, 1)
                if works(k, q, A):
                    reach(pe, d_qk, gA + 1)
                    reach(pe, a_pT, gB + 1)
                    reach(pe, a_x0T, gA + 1)
                    reach(pe, a_mh, gF + 1)
                    for h in range(HEADS):
                        at = slice(HD * (h % 4), HD * (h % 4) + HD)
                        last = nc.tensor.matmul(slot_scores[:, h % 4, h // 4, :], qkT[at, h // 4, :], qkT[at, 2 + h // 4, :],
                                                start=True, stop=True)
                    last.then_inc(p_sc, 1)
                if works(k, q, D):
                    reach(pe, d_tT, gD + 1)
                    reach(pe, d_v2, gD + 1)
                    for c in range(KD):
                        last = nc.tensor.matmul(psD[:, 0:N], tT[:, c, :], x2T[:, c, :], start=(c == 0), stop=(c == KD - 1))
                    last.then_inc(p_s2, 1)
                if works(k, q, C):
                    reach(pe, g_a1T, gC + 1)
                    reach(pe, d_norm[LN1], gC + 1)
                    for c in range(KD):
                        last = nc.tensor.matmul(psC[:, 128 * c:128 * c + 128], x1[:, hC, 128 * c:128 * c + 128], a1T[:, :],
                                                start=True, stop=True)
                    last.then_inc(p_axT, 1)
                if works(k, q, E):
                    reach(pe, g_mx, gE + 1)
                    last = split_product(psE[:, :], mx3Ts, KD, w1T)
                    last.then_inc(p_h, 1)
                if works(k, q, A):
                    reach(pe, g_x0T, gA + 1)
                    reach(pe, d_mask, gA + 1)
                    last = split_product(psA[:, 0:DIM], x0Ts, KD, wvT)
                    last.then_inc(p_v, 1)
                if works(k, q, D):
                    reach(pe, d_w2, gD + 1)
                    nc.tensor.transpose(psD[:, 0:N], w2[:, :], ident[:, :]).then_inc(p_wT, 1)
                if works(k, q, C):
                    reach(pe, g_axT, gC + 1)
                    last = split_product(psC[:, 0:DIM], ax1Ts, KD, w1l)
                    last.then_inc(p_y1, 1)
                if works(k, q, F):
                    reach(pe, g_mh, gF + 1)
                    reach(pe, d_mask, gA + 1)
                    last = split_product(psAF[:, 0:DIM], mhTs, KH, w2T)
                    last.then_inc(p_y3, 1)
                if works(k, q, D):
                    reach(pe, a_wT, gD + 1)
                    reach(pe, d_v2, gD + 1)
                    nc.tensor.matmul(psD[:, 0:DIM], w2dT[:, :], v2[:, 0:DIM], start=True, stop=True).then_inc(p_y2, 1)

            run_steps(pe, step)

        @block.scalar
        def _(act):
            banks = [psA, psAF, psB, psC, psD, psE]
            for n, (dst, _) in enumerate(PREPARED):
                act.wait_ge(s_prep_pe, n + 1)
                src = banks[n % len(banks)][:, :]
                if len(dst.shape) == 3:
                    src = src.rearrange("p (c f) -> p c f", c=2)
                nc.scalar.activation(dst, src, ACT.Copy, scale=2.0 * SCALE if n == 0 else 1.0).then_inc(s_prep_out, 1)
            n = len(PREPARED)
            act.wait_ge(s_prep_pe, n + 1)
            bank = banks[n % len(banks)]
            nc.scalar.activation(t_bias[:, :], bank[:, 0:2], ACT.Copy)
            nc.scalar.activation(wv2T[:, 0, :, DIM:DIM + 2], bank[:, 2:4].unsqueeze(2).to_broadcast([128, KD, 2]), ACT.Copy).then_inc(s_prep_out, 1)
            act.wait_ge(s_prep_pe, n + 2)
            bank = banks[(n + 1) % len(banks)]
            nc.scalar.activation(wa8[:, :], bank[:, 0:DIM], ACT.Copy, scale=0.125).then_inc(s_prep_out, 1)
            act.wait_ge(s_wload[6], 16)
            nc.scalar.activation(w1l[:, 0], w1raw, ACT.Copy).then_inc(s_prep_out, 1)

            def two(t):
                return t[:, 0:2 * N].rearrange("p (c k) -> p c k", c=2)

            def step(k, q):
                i = 2 * k + q
                gA, gB, gC, gD, gE, gF = (i - s for s in range(STAGES))
                hA, hB, hC, hD, hE, hF = ((q - s) % 2 for s in range(STAGES))
                if works(k, q, A):
                    reach(act, p_x0T, gA + 1)
                    reach(act, p_v, gA)
                    nc.scalar.activation(x0T[:, :, :], two(psA), ACT.Copy)
                    nc.scalar.activation(x0Ts[:, 0], two(psA), ACT.Copy).then_inc(a_x0T, 1)
                if works(k, q, B):
                    reach(act, p_pT0, gB + 1)
                    reach(act, p_ctx, gB)
                    nc.scalar.activation(probsT[:, 0:4, :], pT_bank[0], ACT.Copy)
                    reach(act, p_pT1, gB + 1)
                    nc.scalar.activation(probsT[:, 4:8, :], pT_bank[1], ACT.Copy).then_inc(a_pT, 1)
                if works(k, q, D):
                    reach(act, p_x2T, gD + 1)
                    reach(act, p_s2, gD)
                    nc.scalar.activation(x2T[:, :, :], two(psD), ACT.Copy)
                    nc.scalar.activation(x2Ts[:, 0], two(psD), ACT.Copy).then_inc(a_x2T, 1)
                if works(k, q, B):
                    reach(act, p_ctxT, gB + 1)
                    reach(act, p_o, gB)
                    nc.scalar.activation(contextT[:, :, :], two(psB), ACT.Copy)
                    nc.scalar.activation(contextTs[:, 0], two(psB), ACT.Copy).then_inc(a_ctxT, 1)
                if works(k, q, E):
                    reach(act, p_M, gE + 1)
                    reach(act, p_mh, gE - 1)
                    reach(act, d_Dpos, gE - 1)
                    nc.scalar.activation(M[:, hE, :], psE[:, 0:N + 1], ACT.Copy).then_inc(a_M, 1)
                if works(k, q, C):
                    reach(act, p_sT, gC + 1)
                    reach(act, d_leaky, gC)
                    nc.scalar.activation(th[:, :], psC[:, N:2 * N], ACT.Tanh, bias=s8[:, :]).then_inc(a_th, 1)
                    reach(act, g_a1T, gC)
                    nc.scalar.activation(adjCT[:, :], psC[:, 0:N], ACT.Copy).then_inc(a_adjCT, 1)
                if works(k, q, F):
                    reach(act, p_mh, gF + 1)
                    reach(act, p_y3, gF)
                    nc.scalar.activation(mhT[:, :, :], psAF[:, :].rearrange("p (c k) -> p c k", c=KH), ACT.Copy)
                    nc.scalar.activation(mhTs[:, 0], psAF[:, :].rearrange("p (c k) -> p c k", c=KH), ACT.Copy).then_inc(a_mh, 1)
                if works(k, q, C):
                    reach(act, d_leaky, gC + 1)
                    reach(act, d_sumA, gC)
                    nc.scalar.activation(e1[:, :], leaky[:, :], ACT.Exp, scale=8.0).then_inc(a_e1, 1)
                if works(k, q, E):
                    reach(act, p_mx, gE + 1)
                    reach(act, p_h, gE)
                    nc.scalar.activation(mx3T[:, :, :], two(psE), ACT.Copy)
                    nc.scalar.activation(mx3Ts[:, 0], two(psE), ACT.Copy).then_inc(a_mx, 1)
                if works(k, q, C):
                    reach(act, p_axT, gC + 1)
                    reach(act, p_y1, gC)
                    nc.scalar.activation(ax1T[:, :, :], two(psC), ACT.Copy)
                    nc.scalar.activation(ax1Ts[:, 0], two(psC), ACT.Copy).then_inc(a_axT, 1)
                if works(k, q, D):
                    reach(act, p_s2, gD + 1)
                    reach(act, d_v2, gD + 1)
                    reach(act, d_w2, gD)
                    nc.scalar.activation(e2[:, :], psD[:, 0:N], ACT.Exp, bias=v2[:, DIM:DIM + 1]).then_inc(a_e2, 1)
                if works(k, q, A):
                    reach(act, d_max0, gA + 1)
                    reach(act, p_pT1, gA - 1)
                    for slot in range(4):
                        last = nc.scalar.activation(probs[:, hA, slot, :], masked[:, slot, :], ACT.Exp, bias=neg_max[:, slot:slot + 1])
                    last.then_inc(a_exp0, 1)
                if works(k, q, E):
                    reach(act, d_hpre, gE + 1)
                    reach(act, d_norm[LNH], gE)
                    nc.scalar.activation(hrel[:, :], hpre[:, :], ACT.Relu).then_inc(a_relu, 1)
                if works(k, q, D):
                    reach(act, p_wT, gD + 1)
                    reach(act, p_y2, gD)
                    nc.scalar.activation(w2dT[:, :], psD[:, 0:N], ACT.Copy).then_inc(a_wT, 1)
                if works(k, q, A):
                    reach(act, d_max, gA + 1)
                    for slot in range(4, HEADS):
                        last = nc.scalar.activation(probs[:, hA, slot, :], masked[:, slot, :], ACT.Exp, bias=neg_max[:, slot:slot + 1])
                    last.then_inc(a_exp, 1)

            run_steps(act, step)

        @block.vector
        def _(dve):
            nc.vector.memset(v[:, :, :, HD:HD + 1], 1.0)
            dve.wait_ge(s_wload[6], 16)
            dve.wait_ge(s_rows, 16 * BIAS_LOADS)
            for c in range(KD):
                nc.vector.tensor_tensor_reduce(prep_junk[:, :], w1raw[:, c, :], a_row[:, :], 1.0, 0.0, ALU.mult, ALU.add,
                                               wa_col[:, c:c + 1]).then_inc(s_prep_dve, 1)
                dve.wait_ge(s_prep_dve, c + 1)
            nc.vector.tensor_tensor_reduce(prep_junk[:, :], bq2_row[:, :], bk2_row[:, :], 1.0, 0.0, ALU.mult, ALU.add,
                                           bv2_row[:, DIM:DIM + 1]).then_inc(s_prep_dve, 1)
            nc.vector.tensor_scalar(qk_bias[:, 0:2], qk_bias_raw[:, 0:2], 2.0 * SCALE, None, ALU.mult).then_inc(s_prep_dve, 1)
            nc.vector.tensor_copy(qk_bias[:, 2:4], qk_bias_raw[:, 2:4]).then_inc(s_prep_dve, 1)
            banks = [psA, psAF, psB, psC, psD, psE]
            for n, (high, low) in enumerate(PREPARED):
                if low is None:
                    continue
                dve.wait_ge(s_prep_out, n + 1)
                src = banks[n % len(banks)][:, :]
                if len(low.shape) == 3:
                    src = src.rearrange("p (c f) -> p c f", c=2)
                nc.vector.tensor_tensor(low, src, high.bitcast(F32), ALU.subtract).then_inc(s_prep_low, 1)
            n = len(PREPARED)
            dve.wait_ge(s_prep_out, n + 1)
            nc.vector.tensor_tensor(wv2T[:, 1, :, DIM:DIM + 2], banks[n % len(banks)][:, 2:4].unsqueeze(2).to_broadcast([128, KD, 2]),
                                    wv2T[:, 0, :, DIM:DIM + 2].bitcast(F32), ALU.subtract).then_inc(s_prep_low, 1)
            dve.wait_ge(s_prep_out, n + 3)
            nc.vector.tensor_tensor(w1l[:, 1], w1raw, w1l[:, 0].bitcast(F32), ALU.subtract).then_inc(s_prep_low, 1)
            dve.wait_ge(s_prep_dve, KD + 3)

            def norm_stats(n, g, ready, res):
                reach(dve, ready, g + 1)
                reach(dve, d_mv[n], g)
                nc.vector.bn_stats(stats[:, n, :], res[:, :]).then_inc(d_stats[n], 1)

            def norm_mean_var(n, g):
                dve.wait_ge(s_const, 1)
                reach(dve, d_stats[n], g + 1)
                reach(dve, g_vareps[n], g)
                nc.vector.bn_aggr(mv[:, n, :], stats[:, n, :]).then_inc(d_mv[n], 1)

            def norm_apply(n, g, dst, res):
                reach(dve, g_rstd[n], g + 1)
                reach(dve, d_mv[n], g + 1)
                nc.vector.tensor_scalar(dst, res, mv[:, n, 0:1], rstd[:, n, :], ALU.subtract, ALU.mult).then_inc(d_norm[n], 1)

            def mask_head(slot, half):
                return nc.vector.tensor_tensor_reduce(masked[:, slot, :], slot_scores[:, slot // 2, slot % 2, :], adjA[:, half, :],
                                                      1.0, LOWEST, ALU.mult, ALU.max, row_max[:, slot:slot + 1])

            def step(k, q):
                i = 2 * k + q
                gA, gB, gC, gD, gE, gF = (i - s for s in range(STAGES))
                hA, hB, hC, hD, hE, hF = ((q - s) % 2 for s in range(STAGES))
                if works(k, q, E):
                    reach(dve, p_aET, gE + 1)
                    reach(dve, p_M, gE)
                    nc.vector.tensor_scalar(HT[:, :], psE[:, 0:N], 0.0, 0.0, ALU.not_equal, ALU.add,
                                            accum_out=deg[:, 0:1]).then_inc(d_HT, 1)
                if works(k, q, E):
                    reach(dve, p_aET, gE + 1)
                    reach(dve, p_M, gE)
                    nc.vector.tensor_copy(HTB[:, N:N + 1], psE[:, 0:1]).then_inc(d_wedge, 1)
                if works(k, q, C):
                    reach(dve, d_norm[LN1], gC + 1)
                    reach(dve, a_th, gC)
                    reach(dve, p_sT, gC)
                    nc.vector.tensor_tensor_reduce(s_junk[:, :], x1[:, hC, :], wa8[:, :], 1.0, 0.0, ALU.mult, ALU.add,
                                                   s8[:, :]).then_inc(d_s8, 1)
                if works(k, q, E):
                    reach(dve, d_HT, gE + 1)
                    nc.vector.tensor_scalar(deg[:, 1:2], deg[:, 0:1], 1.0, None, ALU.max).then_inc(d_Bg, 1)
                if works(k, q, A):
                    reach16(dve, s_ld_A[hA], k + (q - A) // 2 + 1)
                    reach(dve, p_qk, gA + 1)
                    reach(dve, p_sc, gA)
                    nc.vector.tensor_tensor(qkT[:, :, :], psAF[:, :].rearrange("p (m k) -> p m k", m=4),
                                            qk_bias[:, :].unsqueeze(2).to_broadcast([128, 4, N]), ALU.add).then_inc(d_qk, 1)
                if works(k, q, E):
                    reach(dve, d_Bg, gE + 1)
                    nc.vector.reciprocal(deg[:, 2:3], deg[:, 1:2]).then_inc(d_Binv, 1)
                if works(k, q, C):
                    reach16(dve, s_ld_C[hC], k + (q - C) // 2 + 1)
                    reach(dve, d_ratio, gC)
                    nc.vector.tensor_reduce(sums1[:, 1:2], adjC[:, hC, :], AX.X, ALU.add).then_inc(d_sumadj, 1)
                if works(k, q, B):
                    reach(dve, p_ctx, gB + 1)
                    reach(dve, d_ctx, gB)
                    heads = psB[:, 0:(HD + 1) * HEADS].rearrange("p (h e) -> p h e", h=HEADS)
                    nc.vector.reciprocal(rsum0[:, :, :], heads[:, :, HD:HD + 1]).then_inc(d_rsum0, 1)
                if works(k, q, E):
                    reach(dve, d_Binv, gE + 1)
                    reach(dve, d_wedge, gE + 1)
                    nc.vector.tensor_scalar(HTB[:, 0:N], HT[:, :], deg[:, 2:3], None, ALU.mult).then_inc(d_HTB, 1)
                if works(k, q, B):
                    heads = psB[:, 0:(HD + 1) * HEADS].rearrange("p (h e) -> p h e", h=HEADS)
                    reach(dve, d_rsum0, gB + 1)
                    reach(dve, p_ctxT, gB)
                    nc.vector.tensor_tensor(context[:, :, :], heads[:, :, 0:HD], rsum0[:, :, :].to_broadcast([128, HEADS, HD]),
                                            ALU.mult).then_inc(d_ctx, 1)
                if works(k, q, D):
                    reach(dve, p_tT, gD + 1)
                    reach(dve, p_s2, gD)
                    nc.vector.tensor_tensor(tT[:, :, :], psD[:, 0:DIM].rearrange("p (m k) -> p m k", m=KD),
                                            t_bias[:, :].unsqueeze(2).to_broadcast([128, KD, N]), ALU.add).then_inc(d_tT, 1)
                if works(k, q, E):
                    reach(dve, a_M, gE + 1)
                    reach(dve, d_Dinv, gE)
                    nc.vector.tensor_scalar(deg[:, 3:4], M[:, hE, N:N + 1], 1.17549435e-38, None, ALU.max).then_inc(d_Dg, 1)
                if works(k, q, E):
                    reach(dve, d_Dg, gE + 1)
                    nc.vector.reciprocal(deg[:, 4:5], deg[:, 3:4]).then_inc(d_Drec, 1)
                if works(k, q, C):
                    reach(dve, a_th, gC + 1)
                    reach(dve, a_e1, gC)
                    nc.vector.scalar_tensor_tensor(leaky[:, :], th[:, :], 0.1, th[:, :], ALU.mult, ALU.max).then_inc(d_leaky, 1)
                if works(k, q, B):
                    reach(dve, p_o, gB + 1)
                    reach(dve, g_x0b, gB + 1)
                    reach(dve, d_norm[LN1], gB)
                    nc.vector.tensor_tensor(res1[:, :], psB[:, 0:DIM], x0b[:, hB, :], ALU.add).then_inc(d_res[LN1], 1)
                if works(k, q, D):
                    reach(dve, p_v2, gD + 1)
                    reach(dve, p_y2, gD)
                    reach(dve, a_e2, gD)
                    nc.vector.tensor_tensor(v2[:, :], psD[:, 0:DIM + 1], bv2_row[:, :], ALU.add).then_inc(d_v2, 1)
                if works(k, q, E):
                    reach(dve, a_M, gE + 1)
                    reach(dve, d_Dinv, gE)
                    nc.vector.tensor_scalar(deg[:, 5:6], M[:, hE, N:N + 1], 0.0, None, ALU.is_gt).then_inc(d_Dpos, 1)
                if works(k, q, C):
                    reach(dve, a_e1, gC + 1)
                    reach(dve, d_rA, gC)
                    nc.vector.tensor_tensor_reduce(a1_junk[:, :], e1[:, :], adjC[:, hC, :], 1.0, 0.0, ALU.mult, ALU.add,
                                                   sums1[:, 0:1]).then_inc(d_sumA, 1)
                if works(k, q, E):
                    reach(dve, d_Drec, gE + 1)
                    reach(dve, d_Dpos, gE + 1)
                    reach(dve, d_res[LN4], gE - 1)
                    nc.vector.tensor_tensor(dinv[:, hE, :], deg[:, 4:5], deg[:, 5:6], ALU.mult).then_inc(d_Dinv, 1)
                if works(k, q, E):
                    reach(dve, d_norm[LN3], gE + 1)
                    reach(dve, d_res[LN4], gE - 1)
                    nc.vector.scalar_tensor_tensor(x3b[:, hE, :], x3[:, hE, :], 2.0, b2_row[:, :], ALU.mult, ALU.add).then_inc(d_x3b, 1)
                if works(k, q, B):
                    norm_stats(LN1, gB, d_res[LN1], res1)
                if works(k, q, A):
                    dve.wait_ge(s_const, 1)
                    reach(dve, p_sc, gA + 1)
                    reach(dve, a_exp, gA)
                    for slot in range(4):
                        last = mask_head(slot, hA)
                    last.then_inc(d_mask0, 1)
                if works(k, q, A):
                    for slot in range(4, HEADS):
                        last = mask_head(slot, hA)
                    last.then_inc(d_mask, 1)
                if works(k, q, A):
                    reach(dve, d_mask0, gA + 1)
                    reach(dve, a_exp0, gA)
                    nc.vector.tensor_scalar(neg_max[:, 0:4], row_max[:, 0:4], -1.0, None, ALU.mult).then_inc(d_max0, 1)
                if works(k, q, C):
                    reach(dve, d_sumA, gC + 1)
                    nc.vector.reciprocal(sums1[:, 2:3], sums1[:, 0:1]).then_inc(d_rA, 1)
                if works(k, q, D):
                    reach(dve, a_e2, gD + 1)
                    reach16(dve, s_ld_D[hD], k + (q - D) // 2 + 1)
                    reach(dve, p_wT, gD)
                    reach(dve, d_rden, gD)
                    nc.vector.tensor_tensor_reduce(w2[:, :], e2[:, :], adjD[:, hD, :], 1.0, 0.0, ALU.mult, ALU.add,
                                                   sums2[:, 0:1]).then_inc(d_w2, 1)
                if works(k, q, E):
                    reach(dve, p_h, gE + 1)
                    reach(dve, d_Dinv, gE + 1)
                    reach(dve, a_relu, gE)
                    nc.vector.scalar_tensor_tensor(hpre[:, :], psE[:, :], dinv[:, hE, :], b1_row[:, :], ALU.mult, ALU.add).then_inc(d_hpre, 1)
                if works(k, q, D):
                    reach(dve, d_w2, gD + 1)
                    reach(dve, d_res[LN3], gD)
                    nc.vector.reciprocal(sums2[:, 1:2], sums2[:, 0:1]).then_inc(d_rden, 1)
                if works(k, q, C):
                    reach(dve, d_rA, gC + 1)
                    reach(dve, d_sumadj, gC + 1)
                    reach(dve, d_res[LN2], gC)
                    nc.vector.tensor_tensor(sums1[:, 3:4], sums1[:, 1:2], sums1[:, 2:3], ALU.mult).then_inc(d_ratio, 1)
                if works(k, q, B):
                    norm_mean_var(LN1, gB)
                if works(k, q, A):
                    reach(dve, d_mask, gA + 1)
                    reach(dve, a_exp, gA)
                    nc.vector.tensor_scalar(neg_max[:, 4:8], row_max[:, 4:8], -1.0, None, ALU.mult).then_inc(d_max, 1)
                if works(k, q, A):
                    reach(dve, p_v, gA + 1)
                    reach(dve, p_ctx, gA - 1)
                    nc.vector.tensor_tensor(v[:, hA, :, 0:HD], psA[:, 0:DIM].rearrange("p (h d) -> p h d", h=HEADS),
                                            bv_row[:, :].rearrange("p (h d) -> p h d", h=HEADS), ALU.add).then_inc(d_v, 1)
                if works(k, q, C):
                    reach(dve, p_y1, gC + 1)
                    reach(dve, d_ratio, gC + 1)
                    reach(dve, d_norm[LN2], gC)
                    nc.vector.scalar_tensor_tensor(res2[:, :], psC[:, 0:DIM], sums1[:, 3:4], x1[:, hC, :], ALU.mult, ALU.add).then_inc(d_res[LN2], 1)
                if works(k, q, E):
                    norm_stats(LNH, gE, a_relu, hrel)
                if works(k, q, C):
                    norm_stats(LN2, gC, d_res[LN2], res2)
                if works(k, q, E):
                    norm_mean_var(LNH, gE)
                if works(k, q, F):
                    reach(dve, p_y3, gF + 1)
                    reach(dve, d_x3b, gF + 1)
                    reach(dve, d_norm[LN4], gF)
                    nc.vector.scalar_tensor_tensor(res4[:, :], psAF[:, 0:DIM], dinv[:, hF, :], x3b[:, hF, :], ALU.mult, ALU.add).then_inc(d_res[LN4], 1)
                if works(k, q, C):
                    norm_mean_var(LN2, gC)
                if works(k, q, D):
                    reach(dve, p_y2, gD + 1)
                    reach(dve, d_rden, gD + 1)
                    reach(dve, d_norm[LN3], gD)
                    nc.vector.scalar_tensor_tensor(res3[:, :], psD[:, 0:DIM], sums2[:, 1:2], x2[:, hD, :], ALU.mult, ALU.add).then_inc(d_res[LN3], 1)
                if works(k, q, F):
                    norm_stats(LN4, gF, d_res[LN4], res4)
                if works(k, q, D):
                    norm_stats(LN3, gD, d_res[LN3], res3)
                if works(k, q, F):
                    norm_mean_var(LN4, gF)
                if works(k, q, D):
                    norm_mean_var(LN3, gD)
                if works(k, q, E):
                    reach(dve, g_gam, gE)
                    norm_apply(LNH, gE, hnorm[:, :], hrel[:, :])
                if works(k, q, C):
                    reach(dve, p_x2T, gC - 1)
                    reach(dve, d_res[LN3], gC - 1)
                    norm_apply(LN2, gC, x2[:, hC, :], res2[:, :])
                if works(k, q, B):
                    reach(dve, p_axT, gB - 1)
                    reach(dve, d_res[LN2], gB - 1)
                    norm_apply(LN1, gB, x1[:, hB, :], res1[:, :])
                if works(k, q, F):
                    reach16(dve, s_st[hF], k + (q - F) // 2)
                    norm_apply(LN4, gF, x4[:, hF, :], res4[:, :])
                if works(k, q, D):
                    reach(dve, p_mx, gD - 1)
                    reach(dve, d_x3b, gD - 1)
                    norm_apply(LN3, gD, x3[:, hD, :], res3[:, :])

            run_steps(dve, step)


_INS = ['x', 'adj', 'L0_gnn_Wq', 'L0_gnn_bq', 'L0_gnn_Wk', 'L0_gnn_bk', 'L0_gnn_Wv', 'L0_gnn_bv', 'L0_gnn_Wo', 'L0_gnn_bo',
        'L1_gnn_w', 'L1_gnn_a', 'L2_gnn_Wq_w', 'L2_gnn_Wq_b', 'L2_gnn_Wk_w', 'L2_gnn_Wk_b', 'L2_gnn_Wv_w', 'L2_gnn_Wv_b',
        'L3_gnn_W1', 'L3_gnn_b1', 'L3_gnn_gamma', 'L3_gnn_beta', 'L3_gnn_W2', 'L3_gnn_b2']
_OUTS = [((64, 128, 256), 'float32')]


def kernel(**inputs):
    import numpy as _np
    import concourse.bacc as _bacc
    from concourse import mybir as _mybir
    from concourse.bass_utils import run_bass_kernel_spmd as _run

    nc = _bacc.Bacc("TRN2", target_bir_lowering=False, num_devices=1)
    arrays, args = {}, []
    for name in _INS:
        a = _np.ascontiguousarray(inputs[name])
        arrays[f"in_{name}_dram"] = a
        args.append(nc.dram_tensor(f"in_{name}_dram", a.shape, _mybir.dt.from_np(a.dtype), kind="ExternalInput").ap())
    for i, (shape, dtype) in enumerate(_OUTS):
        dt = _mybir.dt.from_np(_np.dtype(dtype))
        args.append(nc.dram_tensor(f"out_{i}_dram", shape, dt, kind="ExternalOutput").ap())
    pipeline_program(nc, *args)
    r = _run(nc, [arrays], core_ids=[0])
    got = tuple(r.results[0][f"out_{i}_dram"] for i in range(len(_OUTS)))
    return got[0]
```

```python
from contextlib import ExitStack

import concourse.bass as bass
from concourse import mybir

F32 = mybir.dt.float32
F32R = mybir.dt.float32r
ALU = mybir.AluOpType
ACT = mybir.ActivationFunctionType
AX = mybir.AxisListType

A, B, C, D, E, F = range(6)
STORE = STAGES = 6


def pipeline_program(nc, x, adj, Wq, bq, Wk, bk, Wv, bv, Wo, bo, w_l1, a_l1, Wq2, bq2, Wk2, bk2,
                     Wv2, bv2, W1, b1, gamma, beta, W2, b2, out):
    GRAPHS, N, DIM = x.shape
    HID = W1.shape[0]
    HEADS = 8
    HD = DIM // HEADS
    SCALE = float(HD) ** -0.5
    EPS = 1e-5
    LOWEST = -3.4028234e38
    KD = DIM // 128
    KH = HID // 128
    PAIRS = GRAPHS // 2
    assert N == 128 and KD == 2 and KH == 4 and GRAPHS % 2 == 0

    FIRST = STAGES + 2
    LAST = GRAPHS
    END = GRAPHS + STAGES - 1

    with ExitStack() as ctx:
        def sb(name, shape, dt=F32):
            return ctx.enter_context(nc.sbuf_tensor(name, shape, dt))

        def sem(name):
            return ctx.enter_context(nc.semaphore(name))

        ident = sb("ident", [128, 128])
        eps = sb("eps", [128, 1])
        minus_half = sb("minus_half", [128, 1])
        wqT = sb("wqT", [128, KD, DIM])
        wkT = sb("wkT", [128, KD, DIM])
        wvT = sb("wvT", [128, 2, KD, DIM], F32R)
        woT = sb("woT", [128, 2, KD, DIM], F32R)
        w1l = sb("w1l", [128, 2, KD, DIM], F32R)
        wa8 = sb("wa8", [128, DIM])
        gram = sb("gram", [128, KD, DIM])
        wv2T = sb("wv2T", [128, 2, KD, DIM + 2], F32R)
        w1T = sb("w1T", [128, 2, KD, HID], F32R)
        w2T = sb("w2T", [128, 2, KH, DIM], F32R)
        qk_bias = sb("qk_bias", [128, 4])
        t_bias = sb("t_bias", [128, KD])
        bv_row = sb("bv_row", [128, DIM])
        bo_row = sb("bo_row", [128, DIM])
        bv2_row = sb("bv2_row", [128, DIM + 1])
        b1_row = sb("b1_row", [128, HID])
        gamma_row = sb("gamma_row", [128, HID])
        beta_row = sb("beta_row", [128, HID])
        b2_row = sb("b2_row", [128, DIM])
        raw = [sb(f"raw{j}", [128, 1024]) for j in range(7)]
        qk_bias_raw = sb("qk_bias_raw", [128, 4])
        w1raw = raw[6][:, 0:512].rearrange("p (h f) -> p h f", h=KD)
        a_row = sb("a_row", [128, DIM])
        bq2_row = sb("bq2_row", [128, DIM])
        bk2_row = sb("bk2_row", [128, DIM])
        bias2_col = sb("bias2_col", [128, 4])
        wa_col = sb("wa_col", [128, KD])
        prep_junk = sb("prep_junk", [128, DIM])
        act_junk = sb("act_junk", [128, 1])

        x0 = sb("x0", [128, 2, DIM])
        adjA = sb("adjA", [128, 2, N])
        adjC = sb("adjC", [128, 2, N])
        adjD = sb("adjD", [128, 2, N])
        adjE = sb("adjE", [128, 2, N])
        x0T = sb("x0T", [128, KD, N])
        x0Ts = sb("x0Ts", [128, 2, KD, N], F32R)
        qkT = sb("qkT", [128, 4, N])
        v = sb("v", [128, 2, HEADS, HD + 1])
        x0b = sb("x0b", [128, 2, DIM])
        masked = sb("masked", [128, HEADS, N])
        row_max = sb("row_max", [128, HEADS])
        neg_max = sb("neg_max", [128, HEADS])
        probs = sb("probs", [128, 2, HEADS, N])
        probsT = sb("probsT", [128, HEADS, N])
        rsum0 = sb("rsum0", [128, HEADS, 1])
        context = sb("context", [128, HEADS, HD])
        contextT = sb("contextT", [128, KD, N])
        contextTs = sb("contextTs", [128, 2, KD, N], F32R)
        res1 = sb("res1", [128, DIM])
        x1 = sb("x1", [128, 2, DIM])
        s8 = sb("s8", [128, 1])
        s_junk = sb("s_junk", [128, DIM])
        adjCT = sb("adjCT", [128, N])
        th = sb("th", [128, N])
        leaky = sb("leaky", [128, N])
        e1 = sb("e1", [128, N])
        a1T = sb("a1T", [128, N])
        a1_junk = sb("a1_junk", [128, N])
        sums1 = sb("sums1", [128, 4])
        ax1T = sb("ax1T", [128, KD, N])
        ax1Ts = sb("ax1Ts", [128, 2, KD, N], F32R)
        res2 = sb("res2", [128, DIM])
        x2 = sb("x2", [128, 2, DIM])
        x2T = sb("x2T", [128, KD, N])
        x2Ts = sb("x2Ts", [128, 2, KD, N], F32R)
        tT = sb("tT", [128, KD, N])
        v2 = sb("v2", [128, DIM + 1])
        e2 = sb("e2", [128, N])
        w2 = sb("w2", [128, N])
        sums2 = sb("sums2", [128, 2])
        w2dT = sb("w2dT", [128, N])
        res3 = sb("res3", [128, DIM])
        x3 = sb("x3", [128, 2, DIM])
        HT = sb("HT", [128, N])
        HTB = sb("HTB", [128, N + 1])
        deg = sb("deg", [128, 8])
        M = sb("M", [128, 2, N + 1])
        dinv = sb("dinv", [128, 2, 1])
        x3b = sb("x3b", [128, 2, DIM])
        mx3T = sb("mx3T", [128, KD, N])
        mx3Ts = sb("mx3Ts", [128, 2, KD, N], F32R)
        hpre = sb("hpre", [128, HID])
        hrel = sb("hrel", [128, HID])
        hnorm = sb("hnorm", [128, HID])
        hgam = sb("hgam", [128, HID])
        hidden = sb("hidden", [128, 2, HID])
        mhT = sb("mhT", [128, KH, N])
        mhTs = sb("mhTs", [128, 2, KH, N], F32R)
        res4 = sb("res4", [128, DIM])
        x4 = sb("x4", [128, 2, DIM])
        LN1, LN2, LN3, LNH, LN4 = range(5)
        stats = sb("stats", [128, 5, 6])
        mv = sb("mv", [128, 5, 2])
        vareps = sb("vareps", [128, 5, 1])
        rstd = sb("rstd", [128, 5, 1])

        ps = ctx.enter_context(nc.psum_tensor("ps", [128, 8, 512], F32))
        psA, psAF, psB, psC, psD, psE = (ps[:, j, :] for j in range(2, 8))
        slot_scores = ps[:, 0:4, 0:2 * N].rearrange("p b (s k) -> p b s k", s=2)
        SLOTS = [2 * (h % 4) + h // 4 for h in range(HEADS)]
        pT_bank = [ps[:, j, :].rearrange("p (h k) -> p h k", h=HEADS // 2) for j in range(2)]

        s_wload = [sem(f"weights_loaded{j}") for j in range(7)]
        s_rows = {s: sem(f"rows_loaded_{name}") for s, name in ((A, "A"), (C, "C"), (D, "D"), (E, "E"))}
        s_bias2 = sem("bias2_loaded")
        s_qk_bias = sem("qk_bias_set")
        s_wo_load = sem("Wo_loaded")
        s_const = sem("constants_set")
        s_const_pool = sem("pool_constants_set")
        s_prep_pe = sem("prep_products")
        s_prep_out = sem("prep_copied")
        s_prep_dve = sem("prep_vector")
        s_prep_low = sem("prep_low_parts")
        s_w1l_high, s_w1l_low = sem("w1l_high"), sem("w1l_low")

        s_ld_x0 = [sem(f"x0_loaded{q}") for q in range(2)]
        s_ld_A = [sem(f"adjA_loaded{q}") for q in range(2)]
        s_ld_C = [sem(f"adjC_loaded{q}") for q in range(2)]
        s_ld_D = [sem(f"adjD_loaded{q}") for q in range(2)]
        s_ld_E = [sem(f"adjE_loaded{q}") for q in range(2)]
        s_st = [sem(f"out_stored{q}") for q in range(2)]

        p_x0T, p_qk, p_v, p_sc = sem("p_x0T"), sem("p_qk"), sem("p_v"), sem("p_scores")
        p_pT0, p_pT1, p_ctx, p_ctxT, p_o = sem("p_probsT0"), sem("p_probsT1"), sem("p_context"), sem("p_contextT"), sem("p_outproj")
        p_sT, p_axT, p_y1 = sem("p_sT"), sem("p_ax1T"), sem("p_y1")
        p_x2T, p_tT, p_v2, p_s2, p_wT, p_y2 = sem("p_x2T"), sem("p_tT"), sem("p_v2"), sem("p_scores2"), sem("p_w2T"), sem("p_y2")
        p_aET, p_M, p_mx, p_h = sem("p_adjET"), sem("p_M"), sem("p_mx3T"), sem("p_h")
        p_mh, p_y3 = sem("p_mhT"), sem("p_y3")
        a_exp0, a_x0T, a_exp, a_pT, a_ctxT = sem("a_probs0"), sem("a_x0T"), sem("a_probs"), sem("a_probsT"), sem("a_contextT")
        a_adjCT, a_th, a_e1, a_axT = sem("a_adjCT"), sem("a_tanh"), sem("a_e1"), sem("a_ax1T")
        a_x2T, a_e2, a_wT = sem("a_x2T"), sem("a_e2"), sem("a_w2T")
        a_M, a_mx, a_relu, a_mh = sem("a_M"), sem("a_mx3T"), sem("a_relu"), sem("a_mhT")
        d_qk, d_v, d_mask, d_max = sem("d_qk"), sem("d_v"), sem("d_masked"), sem("d_max")
        d_mask0, d_max0 = sem("d_masked0"), sem("d_max0")
        d_x3b = sem("d_x3b")
        d_rsum0, d_ctx = sem("d_rsum0"), sem("d_context")
        d_s8, d_leaky, d_sumA, d_sumadj, d_rA, d_ratio = sem("d_s8"), sem("d_leaky"), sem("d_sumA"), sem("d_sumadj"), sem("d_rA"), sem("d_ratio")
        d_tT, d_v2, d_w2, d_rden = sem("d_tT"), sem("d_v2"), sem("d_w2"), sem("d_rden")
        d_HT, d_wedge, d_Bg, d_Binv, d_HTB = sem("d_HT"), sem("d_wedge"), sem("d_Bguard"), sem("d_Binv"), sem("d_HTB")
        d_Dg, d_Drec, d_Dpos, d_Dinv, d_hpre = sem("d_Dguard"), sem("d_Drec"), sem("d_Dpos"), sem("d_Dinv"), sem("d_hpre")
        d_res = [sem(f"d_res{n}") for n in range(5)]
        d_stats = [sem(f"d_stats{n}") for n in range(5)]
        d_mv = [sem(f"d_mv{n}") for n in range(5)]
        d_norm = [sem(f"d_norm{n}") for n in range(5)]
        g_x0b, g_a1T, g_gam, g_hid = sem("g_x0b"), sem("g_a1T"), sem("g_gamma"), sem("g_hidden")
        g_x0T, g_ctxT, g_axT, g_x2T, g_mx, g_mh = sem("g_x0T"), sem("g_contextT"), sem("g_ax1T"), sem("g_x2T"), sem("g_mx3T"), sem("g_mhT")
        g_vareps = [sem(f"g_vareps{n}") for n in range(5)]
        g_rstd = [sem(f"g_rstd{n}") for n in range(5)]

        def reach(eng, semaphore, count):
            if isinstance(count, int):
                count = min(count, GRAPHS)
                if count < 1:
                    return
            eng.wait_ge(semaphore, count)

        def reach16(eng, semaphore, transfers):
            if isinstance(transfers, int):
                transfers = min(transfers, PAIRS)
                if transfers < 1:
                    return
            eng.wait_ge(semaphore, 16 * transfers)

        def works(k, q, stage):
            return not isinstance(k, int) or 0 <= 2 * k + q - stage < GRAPHS

        def run_steps(eng, step, end=END):
            for i in range(FIRST):
                step(i // 2, i % 2)
            with eng.Fori(FIRST // 2, LAST // 2) as k:
                step(k, 0)
                step(k, 1)
            for i in range(LAST, end):
                step(i // 2, i % 2)

        PREPARED = [
            ((0, 0), psA, wqT[:, :, :], None), ((0, 0), psAF, wkT[:, :, :], None), ((0, 1), psB, wvT[:, 0], wvT[:, 1]),
            ((0, 1), psC, woT[:, 0], woT[:, 1]), ((0, 1), psD, wv2T[:, 0, :, 0:DIM], wv2T[:, 1, :, 0:DIM]),
            ((0, 3), psC, wa8[:, :], None), ((0, 3), psE, gram[:, :, :], None),
            ((0, 3), psD, wv2T[:, 0, :, DIM:DIM + 2], wv2T[:, 1, :, DIM:DIM + 2]), ((1, 1), psE, w1T[:, 0, 0, :], w1T[:, 1, 0, :]),
            ((1, 2), psD, w1T[:, 0, 1, :], w1T[:, 1, 1, :]), ((1, 3), psE, w2T[:, 0, 0:2, :], w2T[:, 1, 0:2, :]),
            ((1, 3), psD, w2T[:, 0, 2:4, :], w2T[:, 1, 2:4, :])]
        QUERY, KEY, VALUE, OUTPROJ, VALUE2, LAYER1_A, GRAM, BIAS2, FIRST_0, FIRST_1, SECOND_0, SECOND_1 = range(12)
        NEEDED = {(0, 0): KEY + 1, (0, 3): VALUE + 1, (1, 0): OUTPROJ + 1, (2, 0): len(PREPARED)}

        def column(src, h):
            return src.rearrange("(h p o) -> h p o", p=128, o=1)[h]

        ROWS = {A: 2 * KD + 2, C: 1, D: 3, E: 4}

        def low_parts(count):
            return sum(low is not None for _, _, _, low in PREPARED[:count])

        def at(k, q, place):
            return (2 * k + q, place) if isinstance(k, int) else None

        def prepares(k, q, place):
            return [n for n, (when, _, _, _) in enumerate(PREPARED) if when == at(k, q, place)]

        block = ctx.enter_context(nc.Block())

        @block.sync
        def _(sp):
            def load(j, at, W, chunks, loaded=None):
                width = W.shape[1]
                sp.dma_start(raw[j][:, at:at + chunks * width].rearrange("p (h d) -> p h d", h=chunks),
                             W.rearrange("(h p) d -> p h d", p=128)).then_inc(loaded or s_wload[j], 16)

            sp.dma_start(x0[:, 0, :], x[0]).then_inc(s_ld_x0[0], 16)
            load(0, 0, Wq, KD)
            load(0, 512, Wk, KD)
            load(1, 0, Wv, KD)
            sp.dma_start(adjA[:, 0, :], adj[0]).then_inc(s_ld_A[0], 16)
            load(1, 512, Wo, KD, s_wo_load)
            load(6, 0, w_l1, KD)
            sp.dma_start(a_row[:, :], a_l1.partition_broadcast(128)).then_inc(s_rows[C], 16)
            load(3, 0, Wv2, KD)
            load(2, 0, Wq2, KD)
            load(2, 512, Wk2, KD)
            for at, src in ((0, bq2), (2, bk2)):
                for h in range(KD):
                    sp.dma_start(bias2_col[:, at + h:at + h + 1], column(src, h)).then_inc(s_bias2, 16)
            load(4, 0, W1, KH)
            load(5, 0, W2, KD)

            def step(k, q):
                i = 2 * k + q
                for stage, dst, src, loaded, used in (
                        (A, x0, x, s_ld_x0, g_x0b), (A, adjA, adj, s_ld_A, d_mask),
                        (C, adjC, adj, s_ld_C, d_sumadj), (D, adjD, adj, s_ld_D, d_w2),
                        (E, adjE, adj, s_ld_E, p_aET)):
                    if not works(k, q, stage) or (isinstance(k, int) and i == 0):
                        continue
                    g, half = i - stage, (q - stage) % 2
                    reach(sp, used, g - 1)
                    if dst is x0:
                        reach(sp, p_x0T, g - 1)
                    if dst is adjC:
                        reach(sp, p_sT, g - 1)
                        reach(sp, d_sumA, g - 1)
                    sp.dma_start(dst[:, half, :], src[g]).then_inc(loaded[half], 16)
                if works(k, q, STORE):
                    reach(sp, d_norm[LN4], i - STORE + 1)
                    sp.dma_start(out[i - STORE], x4[:, (q - STORE) % 2, :]).then_inc(s_st[(q - STORE) % 2], 16)

            run_steps(sp, step, END + 1)
            for q in range(2):
                sp.wait_ge(s_st[q], 16 * PAIRS)

        @block.gpsimd
        def _(pool):
            nc.gpsimd.memset(ident[:, :], 0.0).then_inc(s_const_pool, 1)
            nc.gpsimd.memset(minus_half[:, :], -0.5).then_inc(s_const_pool, 1)
            nc.gpsimd.memset(eps[:, :], EPS).then_inc(s_const_pool, 1)
            pool.wait_ge(s_const_pool, 3)
            nc.gpsimd.affine_select(out=ident[:, :], in_=ident[:, :], compare_op=ALU.not_equal, fill=1.0,
                                    base=0, pattern=[[-1, 128]], channel_multiplier=1).then_inc(s_const, 1)
            for stage, dst, src in ((D, bv2_row[:, 0:DIM], bv2), (D, bq2_row[:, :], bq2), (D, bk2_row[:, :], bk2),
                                    (E, b1_row[:, :], b1), (E, gamma_row[:, :], gamma), (E, beta_row[:, :], beta),
                                    (E, b2_row[:, :], b2)):
                pool.dma_start(dst, src.partition_broadcast(128)).then_inc(s_rows[stage], 16)

            def prepare(k, q, place):
                if at(k, q, place) == (0, 0):
                    pool.wait_ge(s_rows[A], 16 * ROWS[A])
                if at(k, q, place) == (1, 0):
                    pool.wait_ge(s_rows[E], 16 * ROWS[E])

            def add_eps(n, g):
                reach(pool, d_mv[n], g + 1)
                reach(pool, g_rstd[n], g)
                nc.gpsimd.tensor_tensor(vareps[:, n, :], mv[:, n, 1:2], eps[:, :], ALU.add).then_inc(g_vareps[n], 1)

            def power(n, g):
                reach(pool, g_vareps[n], g + 1)
                reach(pool, d_norm[n], g)
                nc.gpsimd.tensor_tensor(rstd[:, n, :], vareps[:, n, :], minus_half[:, :], ALU.pow).then_inc(g_rstd[n], 1)

            def low_part(full, parts, ready, users, done, g):
                reach(pool, ready, g + 1)
                reach(pool, users, g)
                nc.gpsimd.tensor_tensor(parts[:, 1], full[:, :, :], parts[:, 0].bitcast(F32), ALU.subtract).then_inc(done, 1)

            def step(k, q):
                i = 2 * k + q
                prepare(k, q, 0)
                if works(k, q, D):
                    low_part(x2T, x2Ts, a_x2T, p_v2, g_x2T, i - D)
                if works(k, q, C):
                    g, half = i - C, (q - C) % 2
                    reach(pool, a_e1, g + 1)
                    reach(pool, a_adjCT, g + 1)
                    reach(pool, p_axT, g)
                    nc.gpsimd.tensor_tensor(a1T[:, :], e1[:, :], adjCT[:, :], ALU.mult).then_inc(g_a1T, 1)
                if works(k, q, E):
                    low_part(mx3T, mx3Ts, a_mx, p_h, g_mx, i - E)
                if works(k, q, A):
                    low_part(x0T, x0Ts, a_x0T, p_v, g_x0T, i - A)
                if works(k, q, B):
                    low_part(contextT, contextTs, a_ctxT, p_o, g_ctxT, i - B)
                if works(k, q, C):
                    low_part(ax1T, ax1Ts, a_axT, p_y1, g_axT, i - C)
                if works(k, q, F):
                    low_part(mhT, mhTs, a_mh, p_y3, g_mh, i - F)
                if works(k, q, B):
                    add_eps(LN1, i - B)
                if works(k, q, B):
                    power(LN1, i - B)
                if works(k, q, C):
                    add_eps(LN2, i - C)
                if works(k, q, E):
                    add_eps(LNH, i - E)
                if works(k, q, C):
                    power(LN2, i - C)
                if works(k, q, E):
                    power(LNH, i - E)
                if works(k, q, D):
                    add_eps(LN3, i - D)
                if works(k, q, F):
                    add_eps(LN4, i - F)
                if works(k, q, D):
                    power(LN3, i - D)
                if works(k, q, F):
                    power(LN4, i - F)
                if works(k, q, E):
                    g, half = i - E, (q - E) % 2
                    reach(pool, d_norm[LNH], g + 1)
                    reach(pool, g_hid, g)
                    nc.gpsimd.tensor_tensor(hgam[:, :], hnorm[:, :], gamma_row[:, :], ALU.mult).then_inc(g_gam, 1)
                if works(k, q, E):
                    g, half = i - E, (q - E) % 2
                    reach(pool, g_gam, g + 1)
                    reach(pool, p_mh, g - 1)
                    nc.gpsimd.tensor_tensor(hidden[:, half, :], hgam[:, :], beta_row[:, :], ALU.add).then_inc(g_hid, 1)
                if works(k, q, A):
                    g, half = i - A, (q - A) % 2
                    reach16(pool, s_ld_x0[half], k + (q - A) // 2 + 1)
                    reach(pool, d_res[LN1], g - 1)
                    nc.gpsimd.tensor_tensor(x0b[:, half, :], x0[:, half, :], bo_row[:, :], ALU.add).then_inc(g_x0b, 1)

            run_steps(pool, step)

        @block.tensor
        def _(pe):
            pe.wait_ge(s_const, 1)

            def transposed(bank, W, loaded, count, blocks):
                pe.wait_ge(loaded, 16 * count)
                for j, (h, c) in enumerate(blocks):
                    last = nc.tensor.transpose(bank[:, 128 * j:128 * j + 128], W[:, h, 128 * c:128 * c + 128], ident[:, :])
                return last

            def weights(j, at, parts, width=DIM):
                return raw[j][:, at:at + parts * width].rearrange("p (h d) -> p h d", h=parts)

            q2, k2 = weights(2, 0, KD), weights(2, 512, KD)

            def product(n, bank):
                square = [(h, c) for c in range(KD) for h in range(KD)]
                if n == QUERY:
                    return transposed(bank, weights(0, 0, KD), s_wload[0], 2, square)
                if n == KEY:
                    return transposed(bank, weights(0, 512, KD), s_wload[0], 2, square)
                if n == VALUE:
                    return transposed(bank, weights(1, 0, KD), s_wload[1], 1, square)
                if n == OUTPROJ:
                    return transposed(bank, weights(1, 512, KD), s_wo_load, 1, square)
                if n == VALUE2:
                    return transposed(bank, weights(3, 0, KD), s_wload[3], 1, square)
                if n in (FIRST_0, FIRST_1):
                    return transposed(bank, weights(4, 0, KH), s_wload[4], 1, [(h, n - FIRST_0) for h in range(KH)])
                if n in (SECOND_0, SECOND_1):
                    c0 = 2 * (n - SECOND_0)
                    return transposed(bank, weights(5, 0, KD, HID), s_wload[5], 1, [(h, c0 + c) for c in range(2) for h in range(KD)])
                if n == LAYER1_A:
                    pe.wait_ge(s_prep_dve, KD)
                    for c in range(KD):
                        last = nc.tensor.transpose(bank[:, 128 * c:128 * c + 128], wa_col[:, c:c + 1].to_broadcast([128, 128]), ident[:, :])
                    return last
                pe.wait_ge(s_wload[2], 32)
                if n == GRAM:
                    for c in range(KD):
                        for h in range(KD):
                            last = nc.tensor.matmul(bank[:, 256 * c:256 * c + 256], q2[:, h, 128 * c:128 * c + 128], k2[:, h, :],
                                                    start=(h == 0), stop=(h == KD - 1))
                    return last
                pe.wait_ge(s_bias2, 16 * 2 * KD)
                for m, (W, b) in enumerate(((k2, 0), (q2, 2))):
                    for c in range(KD):
                        for h in range(KD):
                            last = nc.tensor.matmul(bank[:, 2 * m + c:2 * m + c + 1], W[:, h, 128 * c:128 * c + 128],
                                                    bias2_col[:, b + h:b + h + 1], start=(h == 0), stop=(h == KD - 1))
                return last

            def prepare(k, q, place):
                for n in prepares(k, q, place):
                    bank = PREPARED[n][1]
                    before = [m for m in range(n) if PREPARED[m][1] is bank]
                    if before:
                        pe.wait_ge(s_prep_out, before[-1] + 1)
                        pe.wait_ge(s_prep_low, low_parts(before[-1] + 1))
                    product(n, bank).then_inc(s_prep_pe, 1)
                if at(k, q, place) in NEEDED:
                    count = NEEDED[at(k, q, place)]
                    pe.wait_ge(s_prep_out, count)
                    if low_parts(count):
                        pe.wait_ge(s_prep_low, low_parts(count))
                    if count == len(PREPARED):
                        pe.wait_ge(s_w1l_low, 1)

            def split_product(dst, parts, chunks, weights):
                terms = [(c, l, r) for l, r in ((0, 0), (0, 1), (1, 0)) for c in range(chunks)]
                for c, l, r in terms:
                    last = nc.tensor.matmul(dst, parts[:, l, c, :], weights[:, r, c, :],
                                            start=((c, l, r) == terms[0]), stop=((c, l, r) == terms[-1]))
                return last

            def step(k, q):
                i = 2 * k + q
                gA, gB, gC, gD, gE, gF = (i - s for s in range(STAGES))
                hA, hB, hC, hD, hE, hF = ((q - s) % 2 for s in range(STAGES))
                prepare(k, q, 0)
                if works(k, q, A):
                    reach16(pe, s_ld_x0[hA], k + (q - A) // 2 + 1)
                    reach(pe, d_v, gA)
                    for c in range(KD):
                        last = nc.tensor.transpose(psA[:, 128 * c:128 * c + 128], x0[:, hA, 128 * c:128 * c + 128], ident[:, :])
                    last.then_inc(p_x0T, 1)
                if works(k, q, E):
                    reach16(pe, s_ld_E[hE], k + (q - E) // 2 + 1)
                    reach(pe, d_hpre, gE)
                    nc.tensor.transpose(psE[:, 0:N], adjE[:, hE, :], ident[:, :]).then_inc(p_aET, 1)
                if works(k, q, B):
                    reach(pe, a_exp, gB + 1)
                    reach(pe, d_mask, gA)
                    for slot in range(HEADS):
                        last = nc.tensor.transpose(pT_bank[slot // 4][:, slot % 4, :], probs[:, hB, slot, :], ident[:, :])
                        if slot == 3:
                            last.then_inc(p_pT0, 1)
                    last.then_inc(p_pT1, 1)
                if works(k, q, A):
                    reach(pe, a_x0T, gA + 1)
                    reach(pe, d_res[LN4], gF)
                    for m, W in enumerate((wqT, wkT)):
                        for f in range(KD):
                            for c in range(KD):
                                last = nc.tensor.matmul(psAF[:, 256 * m + 128 * f:256 * m + 128 * f + 128],
                                                        W[:, c, 128 * f:128 * f + 128], x0T[:, c, :],
                                                        start=(c == 0), stop=(c == KD - 1))
                    last.then_inc(p_qk, 1)
                prepare(k, q, 1)
                if works(k, q, D):
                    reach(pe, d_norm[LN2], gD + 1)
                    reach(pe, d_res[LN3], gD)
                    for c in range(KD):
                        last = nc.tensor.transpose(psD[:, 128 * c:128 * c + 128], x2[:, hD, 128 * c:128 * c + 128], ident[:, :])
                    last.then_inc(p_x2T, 1)
                if works(k, q, B):
                    reach(pe, a_pT, gB + 1)
                    reach(pe, d_v, gB + 1)
                    reach(pe, d_res[LN1], gB)
                    for h in range(HEADS):
                        last = nc.tensor.matmul(psB[:, (HD + 1) * h:(HD + 1) * (h + 1)], probsT[:, SLOTS[h], :], v[:, hB, h, :],
                                                start=True, stop=True)
                    last.then_inc(p_ctx, 1)
                if works(k, q, D):
                    reach(pe, a_x2T, gD + 1)
                    for f in range(KD):
                        for c in range(KD):
                            last = nc.tensor.matmul(psD[:, 128 * f:128 * f + 128], gram[:, c, 128 * f:128 * f + 128], x2T[:, c, :],
                                                    start=(c == 0), stop=(c == KD - 1))
                    last.then_inc(p_tT, 1)
                if works(k, q, E):
                    reach(pe, d_HTB, gE + 1)
                    nc.tensor.matmul(psE[:, 0:N + 1], HT[:, :], HTB[:, :], start=True, stop=True).then_inc(p_M, 1)
                if works(k, q, F):
                    reach(pe, g_hid, gF + 1)
                    reach(pe, a_M, gF + 1)
                    reach(pe, d_qk, gA + 1)
                    for c in range(KH):
                        last = nc.tensor.matmul(psAF[:, 128 * c:128 * c + 128], hidden[:, hF, 128 * c:128 * c + 128], M[:, hF, 0:N],
                                                start=True, stop=True)
                    last.then_inc(p_mh, 1)
                if works(k, q, C):
                    reach(pe, d_s8, gC + 1)
                    reach16(pe, s_ld_C[hC], k + (q - C) // 2 + 1)
                    reach(pe, d_res[LN2], gC)
                    nc.tensor.transpose(psC[:, 0:N], adjC[:, hC, :], ident[:, :])
                    nc.tensor.transpose(psC[:, N:2 * N], s8[:, :].to_broadcast([128, 128]), ident[:, :]).then_inc(p_sT, 1)
                if works(k, q, B):
                    reach(pe, d_ctx, gB + 1)
                    for c in range(KD):
                        last = nc.tensor.transpose(psB[:, 128 * c:128 * c + 128],
                                                   context[:, 4 * c:4 * c + 4, :].rearrange("p h d -> p (h d)"), ident[:, :])
                    last.then_inc(p_ctxT, 1)
                prepare(k, q, 2)
                if works(k, q, E):
                    reach(pe, d_norm[LN3], gE + 1)
                    reach(pe, a_M, gE + 1)
                    for c in range(KD):
                        last = nc.tensor.matmul(psE[:, 128 * c:128 * c + 128], x3[:, hE, 128 * c:128 * c + 128], M[:, hE, 0:N],
                                                start=True, stop=True)
                    last.then_inc(p_mx, 1)
                if works(k, q, D):
                    reach(pe, g_x2T, gD + 1)
                    reach(pe, d_tT, gD + 1)
                    last = split_product(psD[:, 0:DIM + 2], x2Ts, KD, wv2T)
                    last.then_inc(p_v2, 1)
                if works(k, q, A):
                    reach(pe, d_qk, gA + 1)
                    reach(pe, a_pT, gB + 1)
                    reach(pe, a_x0T, gA + 1)
                    reach(pe, a_mh, gF + 1)
                    for h in range(HEADS):
                        at = slice(HD * (h % 4), HD * (h % 4) + HD)
                        last = nc.tensor.matmul(slot_scores[:, h % 4, h // 4, :], qkT[at, h // 4, :], qkT[at, 2 + h // 4, :],
                                                start=True, stop=True)
                    last.then_inc(p_sc, 1)
                prepare(k, q, 3)
                if works(k, q, D):
                    reach(pe, d_tT, gD + 1)
                    reach(pe, d_v2, gD + 1)
                    for c in range(KD):
                        last = nc.tensor.matmul(psD[:, 0:N], tT[:, c, :], x2T[:, c, :], start=(c == 0), stop=(c == KD - 1))
                    last.then_inc(p_s2, 1)
                if works(k, q, C):
                    reach(pe, g_a1T, gC + 1)
                    reach(pe, d_norm[LN1], gC + 1)
                    for c in range(KD):
                        last = nc.tensor.matmul(psC[:, 128 * c:128 * c + 128], x1[:, hC, 128 * c:128 * c + 128], a1T[:, :],
                                                start=True, stop=True)
                    last.then_inc(p_axT, 1)
                if works(k, q, E):
                    reach(pe, g_mx, gE + 1)
                    last = split_product(psE[:, :], mx3Ts, KD, w1T)
                    last.then_inc(p_h, 1)
                if works(k, q, B):
                    reach(pe, g_ctxT, gB + 1)
                    last = split_product(psB[:, 0:DIM], contextTs, KD, woT)
                    last.then_inc(p_o, 1)
                if works(k, q, D):
                    reach(pe, d_w2, gD + 1)
                    nc.tensor.transpose(psD[:, 0:N], w2[:, :], ident[:, :]).then_inc(p_wT, 1)
                if works(k, q, A):
                    reach(pe, g_x0T, gA + 1)
                    reach(pe, d_mask, gA + 1)
                    last = split_product(psA[:, 0:DIM], x0Ts, KD, wvT)
                    last.then_inc(p_v, 1)
                if works(k, q, C):
                    reach(pe, g_axT, gC + 1)
                    last = split_product(psC[:, 0:DIM], ax1Ts, KD, w1l)
                    last.then_inc(p_y1, 1)
                if works(k, q, D):
                    reach(pe, a_wT, gD + 1)
                    reach(pe, d_v2, gD + 1)
                    nc.tensor.matmul(psD[:, 0:DIM], w2dT[:, :], v2[:, 0:DIM], start=True, stop=True).then_inc(p_y2, 1)
                if works(k, q, F):
                    reach(pe, g_mh, gF + 1)
                    reach(pe, d_mask, gA + 1)
                    last = split_product(psAF[:, 0:DIM], mhTs, KH, w2T)
                    last.then_inc(p_y3, 1)

            run_steps(pe, step)

        @block.scalar
        def _(act):
            act.wait_ge(s_const_pool, 3)
            nc.scalar.activation(act_junk[:, :], eps[:, :], ACT.Exp)
            for loaded, dst, src in (
                    *((s_rows[A], qk_bias_raw[:, h:h + 1], column(bq, h)) for h in range(KD)),
                    *((s_rows[A], qk_bias_raw[:, 2 + h:3 + h], column(bk, h)) for h in range(KD)),
                    (s_rows[A], bv_row[:, :], bv.partition_broadcast(128)), (s_rows[A], bo_row[:, :], bo.partition_broadcast(128))):
                act.dma_start(dst, src).then_inc(loaded, 16)

            def prepare(k, q, place):
                for n in prepares(k, q, place):
                    _, bank, high, _ = PREPARED[n]
                    act.wait_ge(s_prep_pe, n + 1)
                    if n == BIAS2:
                        nc.scalar.activation(t_bias[:, :], bank[:, 0:2], ACT.Copy)
                        last = nc.scalar.activation(high, bank[:, 2:4].unsqueeze(2).to_broadcast([128, KD, 2]), ACT.Copy)
                    else:
                        src = bank[:, 0:DIM] if n == LAYER1_A else bank
                        if len(high.shape) == 3:
                            src = src.rearrange("p (c f) -> p c f", c=2)
                        last = nc.scalar.activation(high, src, ACT.Copy, scale={QUERY: 2.0 * SCALE, LAYER1_A: 0.125}.get(n, 1.0))
                    last.then_inc(s_prep_out, 1)
                if at(k, q, place) == (0, 3):
                    act.wait_ge(s_wload[6], 16)
                    nc.scalar.activation(w1l[:, 0], w1raw, ACT.Copy).then_inc(s_w1l_high, 1)

            def two(t):
                return t[:, 0:2 * N].rearrange("p (c k) -> p c k", c=2)

            def step(k, q):
                i = 2 * k + q
                gA, gB, gC, gD, gE, gF = (i - s for s in range(STAGES))
                hA, hB, hC, hD, hE, hF = ((q - s) % 2 for s in range(STAGES))
                prepare(k, q, 0)
                if works(k, q, A):
                    reach(act, p_x0T, gA + 1)
                    reach(act, p_v, gA)
                    nc.scalar.activation(x0T[:, :, :], two(psA), ACT.Copy)
                    nc.scalar.activation(x0Ts[:, 0], two(psA), ACT.Copy).then_inc(a_x0T, 1)
                prepare(k, q, 1)
                if works(k, q, B):
                    reach(act, p_pT0, gB + 1)
                    reach(act, p_ctx, gB)
                    nc.scalar.activation(probsT[:, 0:4, :], pT_bank[0], ACT.Copy)
                    reach(act, p_pT1, gB + 1)
                    nc.scalar.activation(probsT[:, 4:8, :], pT_bank[1], ACT.Copy).then_inc(a_pT, 1)
                if works(k, q, D):
                    reach(act, p_x2T, gD + 1)
                    reach(act, p_s2, gD)
                    nc.scalar.activation(x2T[:, :, :], two(psD), ACT.Copy)
                    nc.scalar.activation(x2Ts[:, 0], two(psD), ACT.Copy).then_inc(a_x2T, 1)
                if works(k, q, E):
                    reach(act, p_M, gE + 1)
                    reach(act, p_mh, gE - 1)
                    reach(act, d_Dpos, gE - 1)
                    nc.scalar.activation(M[:, hE, :], psE[:, 0:N + 1], ACT.Copy).then_inc(a_M, 1)
                if works(k, q, F):
                    reach(act, p_mh, gF + 1)
                    reach(act, p_y3, gF)
                    nc.scalar.activation(mhT[:, :, :], psAF[:, :].rearrange("p (c k) -> p c k", c=KH), ACT.Copy)
                    nc.scalar.activation(mhTs[:, 0], psAF[:, :].rearrange("p (c k) -> p c k", c=KH), ACT.Copy).then_inc(a_mh, 1)
                if works(k, q, C):
                    reach(act, p_sT, gC + 1)
                    reach(act, d_leaky, gC)
                    nc.scalar.activation(th[:, :], psC[:, N:2 * N], ACT.Tanh, bias=s8[:, :]).then_inc(a_th, 1)
                    reach(act, g_a1T, gC)
                    nc.scalar.activation(adjCT[:, :], psC[:, 0:N], ACT.Copy).then_inc(a_adjCT, 1)
                if works(k, q, C):
                    reach(act, d_leaky, gC + 1)
                    reach(act, d_sumA, gC)
                    nc.scalar.activation(e1[:, :], leaky[:, :], ACT.Exp, scale=8.0).then_inc(a_e1, 1)
                if works(k, q, E):
                    reach(act, p_mx, gE + 1)
                    reach(act, p_h, gE)
                    nc.scalar.activation(mx3T[:, :, :], two(psE), ACT.Copy)
                    nc.scalar.activation(mx3Ts[:, 0], two(psE), ACT.Copy).then_inc(a_mx, 1)
                if works(k, q, B):
                    reach(act, p_ctxT, gB + 1)
                    reach(act, p_o, gB)
                    nc.scalar.activation(contextT[:, :, :], two(psB), ACT.Copy)
                    nc.scalar.activation(contextTs[:, 0], two(psB), ACT.Copy).then_inc(a_ctxT, 1)
                prepare(k, q, 2)
                if works(k, q, D):
                    reach(act, p_s2, gD + 1)
                    reach(act, d_v2, gD + 1)
                    reach(act, d_w2, gD)
                    nc.scalar.activation(e2[:, :], psD[:, 0:N], ACT.Exp, bias=v2[:, DIM:DIM + 1]).then_inc(a_e2, 1)
                if works(k, q, C):
                    reach(act, p_axT, gC + 1)
                    reach(act, p_y1, gC)
                    nc.scalar.activation(ax1T[:, :, :], two(psC), ACT.Copy)
                    nc.scalar.activation(ax1Ts[:, 0], two(psC), ACT.Copy).then_inc(a_axT, 1)
                if works(k, q, A):
                    reach(act, d_max0, gA + 1)
                    reach(act, p_pT1, gA - 1)
                    for slot in range(4):
                        last = nc.scalar.activation(probs[:, hA, slot, :], masked[:, slot, :], ACT.Exp, bias=neg_max[:, slot:slot + 1])
                    last.then_inc(a_exp0, 1)
                if works(k, q, D):
                    reach(act, p_wT, gD + 1)
                    reach(act, p_y2, gD)
                    nc.scalar.activation(w2dT[:, :], psD[:, 0:N], ACT.Copy).then_inc(a_wT, 1)
                if works(k, q, E):
                    reach(act, d_hpre, gE + 1)
                    reach(act, d_norm[LNH], gE)
                    nc.scalar.activation(hrel[:, :], hpre[:, :], ACT.Relu).then_inc(a_relu, 1)
                if works(k, q, A):
                    reach(act, d_max, gA + 1)
                    for slot in range(4, HEADS):
                        last = nc.scalar.activation(probs[:, hA, slot, :], masked[:, slot, :], ACT.Exp, bias=neg_max[:, slot:slot + 1])
                    last.then_inc(a_exp, 1)
                prepare(k, q, 3)

            run_steps(act, step)

        @block.vector
        def _(dve):
            nc.vector.memset(v[:, :, :, HD:HD + 1], 1.0)

            def prepare(k, q, place):
                if at(k, q, place) == (0, 0):
                    dve.wait_ge(s_rows[A], 16 * ROWS[A])
                    nc.vector.tensor_scalar(qk_bias[:, 0:2], qk_bias_raw[:, 0:2], 2.0 * SCALE, None, ALU.mult).then_inc(s_qk_bias, 1)
                    nc.vector.tensor_copy(qk_bias[:, 2:4], qk_bias_raw[:, 2:4]).then_inc(s_qk_bias, 1)
                    dve.wait_ge(s_qk_bias, 2)
                if at(k, q, place) == (0, 1):
                    dve.wait_ge(s_wload[6], 16)
                    dve.wait_ge(s_rows[C], 16 * ROWS[C])
                    for c in range(KD):
                        nc.vector.tensor_tensor_reduce(prep_junk[:, :], w1raw[:, c, :], a_row[:, :], 1.0, 0.0, ALU.mult, ALU.add,
                                                       wa_col[:, c:c + 1]).then_inc(s_prep_dve, 1)
                        dve.wait_ge(s_prep_dve, c + 1)
                for n in prepares(k, q, place):
                    _, bank, high, low = PREPARED[n]
                    if low is None:
                        continue
                    dve.wait_ge(s_prep_out, n + 1)
                    if n == BIAS2:
                        src = bank[:, 2:4].unsqueeze(2).to_broadcast([128, KD, 2])
                    else:
                        src = bank if len(low.shape) == 2 else bank.rearrange("p (c f) -> p c f", c=2)
                    nc.vector.tensor_tensor(low, src, high.bitcast(F32), ALU.subtract).then_inc(s_prep_low, 1)
                if at(k, q, place) == (0, 3):
                    dve.wait_ge(s_w1l_high, 1)
                    nc.vector.tensor_tensor(w1l[:, 1], w1raw, w1l[:, 0].bitcast(F32), ALU.subtract).then_inc(s_w1l_low, 1)
                if at(k, q, place) == (1, 3):
                    dve.wait_ge(s_rows[D], 16 * ROWS[D])
                    dve.wait_ge(s_rows[E], 16 * ROWS[E])
                    nc.vector.tensor_tensor_reduce(prep_junk[:, :], bq2_row[:, :], bk2_row[:, :], 1.0, 0.0, ALU.mult, ALU.add,
                                                   bv2_row[:, DIM:DIM + 1]).then_inc(s_prep_dve, 1)
                    dve.wait_ge(s_prep_dve, KD + 1)
                    dve.wait_ge(s_prep_out, len(PREPARED))

            def norm_stats(n, g, ready, res):
                reach(dve, ready, g + 1)
                reach(dve, d_mv[n], g)
                nc.vector.bn_stats(stats[:, n, :], res[:, :]).then_inc(d_stats[n], 1)

            def norm_mean_var(n, g):
                dve.wait_ge(s_const, 1)
                reach(dve, d_stats[n], g + 1)
                reach(dve, g_vareps[n], g)
                nc.vector.bn_aggr(mv[:, n, :], stats[:, n, :]).then_inc(d_mv[n], 1)

            def norm_apply(n, g, dst, res):
                reach(dve, g_rstd[n], g + 1)
                reach(dve, d_mv[n], g + 1)
                nc.vector.tensor_scalar(dst, res, mv[:, n, 0:1], rstd[:, n, :], ALU.subtract, ALU.mult).then_inc(d_norm[n], 1)

            def mask_head(slot, half):
                return nc.vector.tensor_tensor_reduce(masked[:, slot, :], slot_scores[:, slot // 2, slot % 2, :], adjA[:, half, :],
                                                      1.0, LOWEST, ALU.mult, ALU.max, row_max[:, slot:slot + 1])

            def step(k, q):
                i = 2 * k + q
                gA, gB, gC, gD, gE, gF = (i - s for s in range(STAGES))
                hA, hB, hC, hD, hE, hF = ((q - s) % 2 for s in range(STAGES))
                prepare(k, q, 0)
                if works(k, q, E):
                    reach(dve, p_aET, gE + 1)
                    reach(dve, p_M, gE)
                    nc.vector.tensor_scalar(HT[:, :], psE[:, 0:N], 0.0, 0.0, ALU.not_equal, ALU.add,
                                            accum_out=deg[:, 0:1]).then_inc(d_HT, 1)
                if works(k, q, E):
                    reach(dve, p_aET, gE + 1)
                    reach(dve, p_M, gE)
                    nc.vector.tensor_copy(HTB[:, N:N + 1], psE[:, 0:1]).then_inc(d_wedge, 1)
                if works(k, q, A):
                    reach16(dve, s_ld_A[hA], k + (q - A) // 2 + 1)
                    reach(dve, p_qk, gA + 1)
                    reach(dve, p_sc, gA)
                    nc.vector.tensor_tensor(qkT[:, :, :], psAF[:, :].rearrange("p (m k) -> p m k", m=4),
                                            qk_bias[:, :].unsqueeze(2).to_broadcast([128, 4, N]), ALU.add).then_inc(d_qk, 1)
                prepare(k, q, 1)
                if works(k, q, E):
                    reach(dve, d_HT, gE + 1)
                    nc.vector.tensor_scalar(deg[:, 1:2], deg[:, 0:1], 1.0, None, ALU.max).then_inc(d_Bg, 1)
                if works(k, q, E):
                    reach(dve, d_Bg, gE + 1)
                    nc.vector.reciprocal(deg[:, 2:3], deg[:, 1:2]).then_inc(d_Binv, 1)
                if works(k, q, E):
                    reach(dve, d_Binv, gE + 1)
                    reach(dve, d_wedge, gE + 1)
                    nc.vector.tensor_scalar(HTB[:, 0:N], HT[:, :], deg[:, 2:3], None, ALU.mult).then_inc(d_HTB, 1)
                if works(k, q, C):
                    reach(dve, d_norm[LN1], gC + 1)
                    reach(dve, a_th, gC)
                    reach(dve, p_sT, gC)
                    nc.vector.tensor_tensor_reduce(s_junk[:, :], x1[:, hC, :], wa8[:, :], 1.0, 0.0, ALU.mult, ALU.add,
                                                   s8[:, :]).then_inc(d_s8, 1)
                if works(k, q, B):
                    reach(dve, p_ctx, gB + 1)
                    reach(dve, d_ctx, gB)
                    heads = psB[:, 0:(HD + 1) * HEADS].rearrange("p (h e) -> p h e", h=HEADS)
                    nc.vector.reciprocal(rsum0[:, :, :], heads[:, :, HD:HD + 1]).then_inc(d_rsum0, 1)
                if works(k, q, B):
                    heads = psB[:, 0:(HD + 1) * HEADS].rearrange("p (h e) -> p h e", h=HEADS)
                    reach(dve, d_rsum0, gB + 1)
                    reach(dve, p_ctxT, gB)
                    nc.vector.tensor_tensor(context[:, :, :], heads[:, :, 0:HD], rsum0[:, :, :].to_broadcast([128, HEADS, HD]),
                                            ALU.mult).then_inc(d_ctx, 1)
                prepare(k, q, 2)
                if works(k, q, C):
                    reach16(dve, s_ld_C[hC], k + (q - C) // 2 + 1)
                    reach(dve, d_ratio, gC)
                    nc.vector.tensor_reduce(sums1[:, 1:2], adjC[:, hC, :], AX.X, ALU.add).then_inc(d_sumadj, 1)
                if works(k, q, E):
                    reach(dve, d_norm[LN3], gE + 1)
                    reach(dve, d_res[LN4], gE - 1)
                    nc.vector.scalar_tensor_tensor(x3b[:, hE, :], x3[:, hE, :], 2.0, b2_row[:, :], ALU.mult, ALU.add).then_inc(d_x3b, 1)
                if works(k, q, D):
                    reach(dve, p_tT, gD + 1)
                    reach(dve, p_s2, gD)
                    nc.vector.tensor_tensor(tT[:, :, :], psD[:, 0:DIM].rearrange("p (m k) -> p m k", m=KD),
                                            t_bias[:, :].unsqueeze(2).to_broadcast([128, KD, N]), ALU.add).then_inc(d_tT, 1)
                if works(k, q, C):
                    reach(dve, a_th, gC + 1)
                    reach(dve, a_e1, gC)
                    nc.vector.scalar_tensor_tensor(leaky[:, :], th[:, :], 0.1, th[:, :], ALU.mult, ALU.max).then_inc(d_leaky, 1)
                if works(k, q, E):
                    reach(dve, a_M, gE + 1)
                    reach(dve, d_Dinv, gE)
                    nc.vector.tensor_scalar(deg[:, 3:4], M[:, hE, N:N + 1], 1.17549435e-38, None, ALU.max).then_inc(d_Dg, 1)
                if works(k, q, E):
                    reach(dve, d_Dg, gE + 1)
                    nc.vector.reciprocal(deg[:, 4:5], deg[:, 3:4]).then_inc(d_Drec, 1)
                if works(k, q, E):
                    reach(dve, a_M, gE + 1)
                    reach(dve, d_Dinv, gE)
                    nc.vector.tensor_scalar(deg[:, 5:6], M[:, hE, N:N + 1], 0.0, None, ALU.is_gt).then_inc(d_Dpos, 1)
                if works(k, q, D):
                    reach(dve, p_v2, gD + 1)
                    reach(dve, p_y2, gD)
                    reach(dve, a_e2, gD)
                    nc.vector.tensor_tensor(v2[:, :], psD[:, 0:DIM + 1], bv2_row[:, :], ALU.add).then_inc(d_v2, 1)
                if works(k, q, C):
                    reach(dve, a_e1, gC + 1)
                    reach(dve, d_rA, gC)
                    nc.vector.tensor_tensor_reduce(a1_junk[:, :], e1[:, :], adjC[:, hC, :], 1.0, 0.0, ALU.mult, ALU.add,
                                                   sums1[:, 0:1]).then_inc(d_sumA, 1)
                if works(k, q, C):
                    reach(dve, d_sumA, gC + 1)
                    nc.vector.reciprocal(sums1[:, 2:3], sums1[:, 0:1]).then_inc(d_rA, 1)
                if works(k, q, E):
                    reach(dve, d_Drec, gE + 1)
                    reach(dve, d_Dpos, gE + 1)
                    reach(dve, d_res[LN4], gE - 1)
                    nc.vector.tensor_tensor(dinv[:, hE, :], deg[:, 4:5], deg[:, 5:6], ALU.mult).then_inc(d_Dinv, 1)
                if works(k, q, A):
                    dve.wait_ge(s_const, 1)
                    reach(dve, p_sc, gA + 1)
                    reach(dve, a_exp, gA)
                    for slot in range(4):
                        last = mask_head(slot, hA)
                    last.then_inc(d_mask0, 1)
                if works(k, q, D):
                    reach(dve, a_e2, gD + 1)
                    reach16(dve, s_ld_D[hD], k + (q - D) // 2 + 1)
                    reach(dve, p_wT, gD)
                    reach(dve, d_rden, gD)
                    nc.vector.tensor_tensor_reduce(w2[:, :], e2[:, :], adjD[:, hD, :], 1.0, 0.0, ALU.mult, ALU.add,
                                                   sums2[:, 0:1]).then_inc(d_w2, 1)
                if works(k, q, A):
                    reach(dve, d_mask0, gA + 1)
                    reach(dve, a_exp0, gA)
                    nc.vector.tensor_scalar(neg_max[:, 0:4], row_max[:, 0:4], -1.0, None, ALU.mult).then_inc(d_max0, 1)
                if works(k, q, A):
                    for slot in range(4, HEADS):
                        last = mask_head(slot, hA)
                    last.then_inc(d_mask, 1)
                if works(k, q, D):
                    reach(dve, d_w2, gD + 1)
                    reach(dve, d_res[LN3], gD)
                    nc.vector.reciprocal(sums2[:, 1:2], sums2[:, 0:1]).then_inc(d_rden, 1)
                if works(k, q, C):
                    reach(dve, d_rA, gC + 1)
                    reach(dve, d_sumadj, gC + 1)
                    reach(dve, d_res[LN2], gC)
                    nc.vector.tensor_tensor(sums1[:, 3:4], sums1[:, 1:2], sums1[:, 2:3], ALU.mult).then_inc(d_ratio, 1)
                if works(k, q, E):
                    reach(dve, p_h, gE + 1)
                    reach(dve, d_Dinv, gE + 1)
                    reach(dve, a_relu, gE)
                    nc.vector.scalar_tensor_tensor(hpre[:, :], psE[:, :], dinv[:, hE, :], b1_row[:, :], ALU.mult, ALU.add).then_inc(d_hpre, 1)
                if works(k, q, A):
                    reach(dve, d_mask, gA + 1)
                    reach(dve, a_exp, gA)
                    nc.vector.tensor_scalar(neg_max[:, 4:8], row_max[:, 4:8], -1.0, None, ALU.mult).then_inc(d_max, 1)
                if works(k, q, B):
                    reach(dve, p_o, gB + 1)
                    reach(dve, g_x0b, gB + 1)
                    reach(dve, d_norm[LN1], gB)
                    nc.vector.tensor_tensor(res1[:, :], psB[:, 0:DIM], x0b[:, hB, :], ALU.add).then_inc(d_res[LN1], 1)
                if works(k, q, B):
                    norm_stats(LN1, gB, d_res[LN1], res1)
                if works(k, q, A):
                    reach(dve, p_v, gA + 1)
                    reach(dve, p_ctx, gA - 1)
                    nc.vector.tensor_tensor(v[:, hA, :, 0:HD], psA[:, 0:DIM].rearrange("p (h d) -> p h d", h=HEADS),
                                            bv_row[:, :].rearrange("p (h d) -> p h d", h=HEADS), ALU.add).then_inc(d_v, 1)
                prepare(k, q, 3)
                if works(k, q, B):
                    norm_mean_var(LN1, gB)
                if works(k, q, C):
                    reach(dve, p_y1, gC + 1)
                    reach(dve, d_ratio, gC + 1)
                    reach(dve, d_norm[LN2], gC)
                    nc.vector.scalar_tensor_tensor(res2[:, :], psC[:, 0:DIM], sums1[:, 3:4], x1[:, hC, :], ALU.mult, ALU.add).then_inc(d_res[LN2], 1)
                if works(k, q, E):
                    norm_stats(LNH, gE, a_relu, hrel)
                if works(k, q, C):
                    norm_stats(LN2, gC, d_res[LN2], res2)
                if works(k, q, D):
                    reach(dve, p_y2, gD + 1)
                    reach(dve, d_rden, gD + 1)
                    reach(dve, d_norm[LN3], gD)
                    nc.vector.scalar_tensor_tensor(res3[:, :], psD[:, 0:DIM], sums2[:, 1:2], x2[:, hD, :], ALU.mult, ALU.add).then_inc(d_res[LN3], 1)
                if works(k, q, C):
                    norm_mean_var(LN2, gC)
                if works(k, q, E):
                    norm_mean_var(LNH, gE)
                if works(k, q, F):
                    reach(dve, p_y3, gF + 1)
                    reach(dve, d_x3b, gF + 1)
                    reach(dve, d_norm[LN4], gF)
                    nc.vector.scalar_tensor_tensor(res4[:, :], psAF[:, 0:DIM], dinv[:, hF, :], x3b[:, hF, :], ALU.mult, ALU.add).then_inc(d_res[LN4], 1)
                if works(k, q, D):
                    norm_stats(LN3, gD, d_res[LN3], res3)
                if works(k, q, F):
                    norm_stats(LN4, gF, d_res[LN4], res4)
                if works(k, q, D):
                    norm_mean_var(LN3, gD)
                if works(k, q, F):
                    norm_mean_var(LN4, gF)
                if works(k, q, C):
                    reach(dve, p_x2T, gC - 1)
                    reach(dve, d_res[LN3], gC - 1)
                    norm_apply(LN2, gC, x2[:, hC, :], res2[:, :])
                if works(k, q, E):
                    reach(dve, g_gam, gE)
                    norm_apply(LNH, gE, hnorm[:, :], hrel[:, :])
                if works(k, q, B):
                    reach(dve, p_axT, gB - 1)
                    reach(dve, d_res[LN2], gB - 1)
                    norm_apply(LN1, gB, x1[:, hB, :], res1[:, :])
                if works(k, q, D):
                    reach(dve, p_mx, gD - 1)
                    reach(dve, d_x3b, gD - 1)
                    norm_apply(LN3, gD, x3[:, hD, :], res3[:, :])
                if works(k, q, F):
                    reach16(dve, s_st[hF], k + (q - F) // 2)
                    norm_apply(LN4, gF, x4[:, hF, :], res4[:, :])

            run_steps(dve, step)


_INS = ['x', 'adj', 'L0_gnn_Wq', 'L0_gnn_bq', 'L0_gnn_Wk', 'L0_gnn_bk', 'L0_gnn_Wv', 'L0_gnn_bv', 'L0_gnn_Wo', 'L0_gnn_bo',
        'L1_gnn_w', 'L1_gnn_a', 'L2_gnn_Wq_w', 'L2_gnn_Wq_b', 'L2_gnn_Wk_w', 'L2_gnn_Wk_b', 'L2_gnn_Wv_w', 'L2_gnn_Wv_b',
        'L3_gnn_W1', 'L3_gnn_b1', 'L3_gnn_gamma', 'L3_gnn_beta', 'L3_gnn_W2', 'L3_gnn_b2']
_OUTS = [((64, 128, 256), 'float32')]


def kernel(**inputs):
    import numpy as _np
    import concourse.bacc as _bacc
    from concourse import mybir as _mybir
    from concourse.bass_utils import run_bass_kernel_spmd as _run

    nc = _bacc.Bacc("TRN2", target_bir_lowering=False, num_devices=1)
    arrays, args = {}, []
    for name in _INS:
        a = _np.ascontiguousarray(inputs[name])
        arrays[f"in_{name}_dram"] = a
        args.append(nc.dram_tensor(f"in_{name}_dram", a.shape, _mybir.dt.from_np(a.dtype), kind="ExternalInput").ap())
    for i, (shape, dtype) in enumerate(_OUTS):
        dt = _mybir.dt.from_np(_np.dtype(dtype))
        args.append(nc.dram_tensor(f"out_{i}_dram", shape, dt, kind="ExternalOutput").ap())
    pipeline_program(nc, *args)
    r = _run(nc, [arrays], core_ids=[0])
    got = tuple(r.results[0][f"out_{i}_dram"] for i in range(len(_OUTS)))
    return got[0]
```
